# Optimizing a Trainium2 kernel written in Bass

```python
import numpy as np
import jax
import jax.numpy as jnp

def _softmax(x, axis=-1):
    return jax.nn.softmax(x, axis=axis)

def _gelu(x):
    return jax.nn.gelu(x, approximate=True)

def _silu(x):
    return jax.nn.silu(x)

def _sigmoid(x):
    return jax.nn.sigmoid(x)

def _layernorm(x, axis=-1, eps=1e-05):
    m = jnp.mean(x, axis=axis, keepdims=True)
    v = jnp.var(x, axis=axis, keepdims=True)
    return (x - m) / jnp.sqrt(v + eps)

def _scatter_add(tgt, idx, src, axis=0):
    return tgt.at[idx].add(src)

def _segment_sum(src, seg, n):
    return jax.ops.segment_sum(src, seg, n)
kernel_name = 'mk_seq_postln_d1_jaxref_r8_b17c87'

def setup_inputs(seed: int=0):
    np.random.seed(seed)
    _w = jnp.asarray

    def _L0_attn_setup():
        import jax, jax.numpy as jnp
        import numpy as np
        B, N, D = (8, 128, 512)
        H = 8
        HEAD_DIM = D // H
        E = HEAD_DIM // H
        key = jax.random.key(seed)
        ks = jax.random.split(key, 7)
        s = 0.02
        return {'x': jax.random.normal(ks[0], (B, N, D), dtype=jnp.float32), 'Wqk_w': jax.random.normal(ks[1], (2 * HEAD_DIM, D), dtype=jnp.float32) * s, 'Wqk_b': jnp.zeros((2 * HEAD_DIM,), dtype=jnp.float32), 'Wv_w': jax.random.normal(ks[2], (HEAD_DIM, D), dtype=jnp.float32) * s, 'Wv_b': jnp.zeros((HEAD_DIM,), dtype=jnp.float32), 'Wo_w': jax.random.normal(ks[3], (D, HEAD_DIM), dtype=jnp.float32) * s, 'Wo_b': jnp.zeros((D,), dtype=jnp.float32)}
    _L0_attn_in = _L0_attn_setup()

    def _L0_ffn_setup():
        import jax, jax.numpy as jnp
        import numpy as np
        H = 512
        I = 1792
        G = 128

        def dequant(q, s, g=G):
            O, In = q.shape
            return (q.reshape(O, In // g, g).astype(s.dtype) * s[:, :, None]).reshape(O, In)
        key = jax.random.key(seed)
        ks = jax.random.split(key, 7)
        x = jax.random.normal(ks[0], (2, 256, H), dtype=jnp.float32)

        def mk_qlinear(kq, ksc, out_d, in_d):
            q = jax.random.randint(kq, (out_d, in_d), -8, 8, dtype=jnp.int32)
            s = jax.random.uniform(ksc, (out_d, in_d // G), dtype=jnp.float32, minval=0.005, maxval=0.02)
            return (q, s)
        gate_q, gate_s = mk_qlinear(ks[1], ks[2], I, H)
        up_q, up_s = mk_qlinear(ks[3], ks[4], I, H)
        down_q, down_s = mk_qlinear(ks[5], ks[6], H, I)
        return {'x': x, 'gate_q': gate_q, 'gate_s': gate_s, 'up_q': up_q, 'up_s': up_s, 'down_q': down_q, 'down_s': down_s}
    _L0_ffn_in = _L0_ffn_setup()
    _d = {'L0_attn_x': _L0_attn_in['x'], 'L0_attn_Wqk_w': _L0_attn_in['Wqk_w'], 'L0_attn_Wqk_b': _L0_attn_in['Wqk_b'], 'L0_attn_Wv_w': _L0_attn_in['Wv_w'], 'L0_attn_Wv_b': _L0_attn_in['Wv_b'], 'L0_attn_Wo_w': _L0_attn_in['Wo_w'], 'L0_attn_Wo_b': _L0_attn_in['Wo_b'], 'L0_ffn_gate_q': _L0_ffn_in['gate_q'], 'L0_ffn_gate_s': _L0_ffn_in['gate_s'], 'L0_ffn_up_q': _L0_ffn_in['up_q'], 'L0_ffn_up_s': _L0_ffn_in['up_s'], 'L0_ffn_down_q': _L0_ffn_in['down_q'], 'L0_ffn_down_s': _L0_ffn_in['down_s']}
    _x0 = _d['L0_attn_x']
    _d['L0_attn_x'] = jax.random.normal(jax.random.fold_in(jax.random.key(seed), 1), (2, 1024, 512), dtype=_x0.dtype)
    del _x0
    return _d

def reference(L0_attn_x, L0_attn_Wqk_w, L0_attn_Wqk_b, L0_attn_Wv_w, L0_attn_Wv_b, L0_attn_Wo_w, L0_attn_Wo_b, L0_ffn_gate_q, L0_ffn_gate_s, L0_ffn_up_q, L0_ffn_up_s, L0_ffn_down_q, L0_ffn_down_s):

    def _L0_attn_ref(x, Wqk_w, Wqk_b, Wv_w, Wv_b, Wo_w, Wo_b):
        import jax, jax.numpy as jnp
        import numpy as np
        B, N, D = (8, 128, 512)
        H = 8
        HEAD_DIM = D // H
        E = HEAD_DIM // H
        b, n, _ = x.shape
        qk = (x @ Wqk_w.T + Wqk_b).reshape(b, n, H, E, 2)
        q = jnp.transpose(qk[..., 0], (0, 2, 1, 3))
        k = jnp.transpose(qk[..., 1], (0, 2, 1, 3))
        v = (x @ Wv_w.T + Wv_b).reshape(b, n, H, E)
        v = jnp.transpose(v, (0, 2, 1, 3))
        scores = jnp.einsum('bhqd,bhkd->bhqk', q, k)
        attn = jax.nn.softmax(scores, axis=-1) / jnp.asarray(HEAD_DIM ** 0.5, x.dtype)
        out = jnp.einsum('bhsl,bhlv->bhsv', attn, v)
        out = jnp.transpose(out, (0, 2, 1, 3)).reshape(b, n, H * E)
        return out @ Wo_w.T + Wo_b

    def _L0_ffn_ref(x, gate_q, gate_s, up_q, up_s, down_q, down_s):
        import jax, jax.numpy as jnp
        import numpy as np
        H = 512
        I = 1792
        G = 128

        def dequant(q, s, g=G):
            O, In = q.shape
            return (q.reshape(O, In // g, g).astype(s.dtype) * s[:, :, None]).reshape(O, In)
        Wg = dequant(gate_q, gate_s)
        Wu = dequant(up_q, up_s)
        Wd = dequant(down_q, down_s)
        gate_score = jax.nn.silu(jnp.einsum('bsh,ih->bsi', x, Wg))
        intermediate = gate_score * jnp.einsum('bsh,ih->bsi', x, Wu)
        return jnp.einsum('bsi,hi->bsh', intermediate, Wd)
    x = L0_attn_x
    x = _layernorm(x + _L0_attn_ref(x, L0_attn_Wqk_w, L0_attn_Wqk_b, L0_attn_Wv_w, L0_attn_Wv_b, L0_attn_Wo_w, L0_attn_Wo_b), axis=-1)
    x = _layernorm(x + _L0_ffn_ref(x, L0_ffn_gate_q, L0_ffn_gate_s, L0_ffn_up_q, L0_ffn_up_s, L0_ffn_down_q, L0_ffn_down_s), axis=-1)
    return x

_drawn_inputs = setup_inputs


def setup_inputs(seed=0):
    import zlib

    import numpy as np

    out = dict(_drawn_inputs(seed))
    spreads = {'L0_attn_Wqk_b': (0.0, 0.8), 'L0_attn_Wv_b': (0.0, 0.8), 'L0_attn_Wo_b': (0.0, 0.1)}
    factors = {'L0_attn_Wqk_w': 8.0, 'L0_attn_Wv_w': 8.0, 'L0_attn_Wo_w': 8.0}
    for name, (base, spread) in spreads.items():
        noise = np.random.default_rng([zlib.crc32(name.encode()), seed]).standard_normal(out[name].shape)
        drawn = base * np.exp(spread * noise) if base else spread * noise
        out[name] = jnp.asarray(drawn.astype(out[name].dtype))
    for name, factor in factors.items():
        out[name] = (out[name] * factor).astype(out[name].dtype)
    return out
```

```python
from contextlib import ExitStack

import numpy as np
import concourse.bass as bass
from concourse import mybir

ALU = mybir.AluOpType
ACT = mybir.ActivationFunctionType
F32 = mybir.dt.float32
F16 = mybir.dt.float16
BF16 = mybir.dt.bfloat16
I32 = mybir.dt.int32
AX = mybir.AxisListType

P = 128
B, N, D = 2, 1024, 512
T = B * N
H, E = 8, 8
HD = H * E
I = 1792
C = D // P
G = I // P
TB = 512
NB = T // TB
BT = TB // P
KT = N // P
SLOTS = 12
KR = SLOTS * E
MROW = 9 * E
VC = 32
HG = 4
NG = H // HG
STEPS = NG * KT
EPS = 1e-5
WSCALE = 1024.0
ONES2 = float(np.array([0x3F803F80], np.uint32).view(np.float32)[0])


def build(nc, x, xT, wqkT, bqk, wvT, bv, woT, gq, gs, uq, us, dq, ds, out):
    ctx = ExitStack()
    with ctx:
        def sb(name, shape, dt):
            return ctx.enter_context(nc.sbuf_tensor(name, shape, dt))

        def sem(name):
            return ctx.enter_context(nc.semaphore(name))

        stack = [sb(f"stack{b}", [P, 2, H * N], BF16) for b in range(B)]
        ks = [stack[b][0:KR, 0, :].rearrange("p (h n) -> p h n", h=H) for b in range(B)]
        qs = [stack[b][0:KR, 1, :].rearrange("p (k h n) -> p k h n", k=N // TB, h=H) for b in range(B)]
        wd = stack[0][:, :, 0:G * D].bitcast(F16).rearrange("p s (g n) -> p s g n", g=G)
        NM = 3
        mparts = stack[1][:, 0, 0:2 * NM * TB].bitcast(F16).rearrange("p (s k n) -> p s k n", s=2, k=NM)
        arena = sb("arena", [P, NB, C * TB], F32)
        xt = [arena[:, k, :].rearrange("p (c n) -> p c n", c=C) for k in range(2)]
        vst = [arena[:, 2 + b, :].rearrange("p (k h v) -> p k h v", k=KT, h=H) for b in range(B)]
        x1t = [arena[:, k, :].bitcast(F16).rearrange("p (s c n) -> p s c n", s=2, c=C) for k in range(NB)]
        x1 = sb("x1", [P, T // P, D], F32)
        qkf = x1[:, 8:10, :].rearrange("p a n -> p (a n)")
        res1 = x1[:, 10:12, :].rearrange("p a n -> p (a n)")
        part = [x1[:, 12 + i, :].bitcast(BF16) for i in range(3)]
        vtmp = x1[:, 15, :]
        wg = sb("wg", [P, C, I], F16)
        wu = sb("wu", [P, C, I], F16)
        pbuf = sb("pbuf", [P, 4, 2 * TB], F32)
        tmp = pbuf[:, :, :].rearrange("p a (b n) -> p (a b) n", b=2)
        ag, au, sg = [tmp[:, 0 + k, :] for k in range(2)], [tmp[:, 2 + k, :] for k in range(2)], \
            [tmp[:, 4 + k, :] for k in range(2)]
        dqs = sb("dqs", [P, 2, D], F16)
        dsb = sb("dsb", [P, 2, D], F32)
        w32 = sb("w32", [P, D], F32)
        sdr = sb("sdr", [G, D], F32)
        sds = sb("sds", [G, D], F32)
        wqk_s = sb("wqk_s", [P, C, 2 * HD], F32)
        wv_s = sb("wv_s", [P, C, HD], F32)
        wo_s = sb("wo_s", [KR, D], F32)
        bqk_s = sb("bqk_s", [P, 1], F32)
        bv_s = sb("bv_s", [P, 1], F32)
        gs_s = sb("gs_s", [P, G, C], F32)
        us_s = sb("us_s", [P, G, C], F32)
        ident = sb("ident", [P, P], F32)
        eps = sb("eps", [P, 1], F32)
        avt = sb("avt", [P, 2, TB], F32)
        att = sb("att", [P, BT, KR], F32)
        attT = sb("attT", [KR, TB], F32)
        rec = sb("rec", [P, BT, HG], F32)
        mxh = sb("mxh", [P, 2, HG * BT, 2], F32)
        mx = sb("mx", [P, 2, HG * BT], F32)
        negm = sb("negm", [HG * BT, P], F32)
        mres = sb("mres", [HG * BT, 2, P], F32)
        mp = sb("mp", [HG * BT, 2, 3, P], BF16)
        st = sb("st", [P, BT, 6], F32)
        mv = sb("mv", [P, BT, 2], F32)
        sd = sb("sd", [P, BT], F32)
        rstd = sb("rstd", [P, BT], F32)

        ps = ctx.enter_context(nc.psum_tensor("ps", [P, 8, TB], F32))
        bank = [ps[:, k, :] for k in range(8)]
        MAXB, AVB, MISC, GUB = 4, 6, 7, 4
        ds_scaled = nc.dram_tensor("ds_scaled", [G, D], F32, kind="Internal").ap()

        s_xt = [sem(f"xt_loaded{k}") for k in range(2)]
        s_w = sem("attn_weights_loaded")
        s_x = [sem(f"x_loaded{b}") for b in range(B)]
        s_gu = sem("gate_up_loaded")
        s_sc = sem("gate_up_scales_loaded")
        s_sdr = sem("down_scales_loaded")
        s_sds = sem("down_scales_multiplied")
        s_sdd = sem("down_scales_stored")
        s_dq = [sem(f"down_q_loaded{k}") for k in range(2)]
        s_dsb = [sem(f"down_scales_spread{k}") for k in range(2)]
        s_id = sem("identity_ready")
        s_fill = sem("stack_rows_filled")
        s_zero = sem("v_zeroed")
        s_const = sem("constants_set")
        s_proj = sem("projection_full")
        s_projr = sem("projection_read")
        s_vt = sem("v_transposed")
        s_vc = sem("v_placed")
        s_split = sem("qk_residual_ready")
        s_parts = sem("qk_parts_ready")
        s_stk = [sem(f"stack_loaded{b}") for b in range(B)]
        s_mxf = sem("max_scores_full")
        s_mxr = sem("max_scores_read")
        s_mxc = sem("maxima_combined")
        s_msp = sem("maxima_split")
        s_mrow = sem("max_parts_ready")
        s_mld = [sem(f"max_rows_in_stack{g}") for g in range(NG)]
        s_scf = sem("scores_full")
        s_exp = sem("exp_done")
        s_av = sem("av_step_done")
        s_ave = sem("av_evacuated")
        s_mf = sem("misc_full")
        s_mr = sem("misc_read")
        s_rec = sem("denominators_inverted")
        s_bn = sem("ln_stats_of_tile")
        s_st = sem("ln_mean_variance_ready")
        s_sd = sem("ln_deviation_ready")
        s_rstd = sem("ln_inverse_ready")
        s_x1 = sem("x1_ready")
        s_hi = sem("x1t_high_ready")
        s_w32 = sem("down_weights_dequantised")
        s_wh = sem("down_weights_high_ready")
        s_wl = sem("down_weights_low_ready")
        s_guf = sem("gate_up_full")
        s_a0 = sem("first_group_scaled")
        s_gud = sem("group_added")
        s_silu = sem("silu_done")
        s_mul = sem("inner_ready")
        s_mh = sem("inner_high_ready")
        s_ml = sem("inner_low_ready")
        s_dn = sem("down_tile_done")
        s_y = sem("down_added")
        s_res = sem("result_ready")
        s_out = sem("output_stored")

        block = ctx.enter_context(nc.Block())

        def misc_at(u, s):
            uses = []
            if u < NB and s == 1:
                uses.append(("M", u, 1))
            if u + 1 < NB and s == 9:
                uses.append(("M", u + 1, 0))
            if u < NB and s == 11:
                uses.append(("avT", u, 0))
            if u > 0:
                if s == 2:
                    uses.append(("avT", u - 1, 1))
                if s == 3:
                    uses.append(("attT", u - 1, 0))
                if 5 <= s < 5 + BT:
                    uses.append(("wo", u - 1, s - 5))
                if STEPS - C <= s:
                    uses.append(("x1T", u - 1, s - STEPS + C))
            return uses

        misc_order = [("M", 0, 0)] + [use for u in range(NB + 1) for s in range(STEPS) for use in misc_at(u, s)]

        def misc_count(*use):
            return misc_order.index(use) + 1

        @block.sync
        def _(sp):
            for k in range(2):
                sp.dma_start(xt[k], xT[:, :, k * TB:(k + 1) * TB].rearrange("c p n -> p c n")).then_inc(s_xt[k], 16)
                if k == 0:
                    sp.dma_start(wqk_s[:], wqkT).then_inc(s_w, 16)
                    sp.dma_start(bqk_s[:], bqk).then_inc(s_w, 16)
                    sp.dma_start(wv_s[:], wvT).then_inc(s_w, 16)
                    sp.dma_start(bv_s[:], bv).then_inc(s_w, 16)
            sp.dma_start(wo_s[:], woT).then_inc(s_w, 16)

            def stacks(b):
                sp.wait_ge(s_fill, 4)
                for i in range(3):
                    sp.wait_ge(s_parts, 3 * b + i + 1)
                    for j in range(3):
                        r = 3 * i + j
                        for k in range(N // TB):
                            sp.dma_start(qs[b][r * E:(r + 1) * E, k, :, :],
                                         part[i][0:HD, k * TB:(k + 1) * TB]).then_inc(s_stk[b], 16)
                        r = 3 * j + i
                        sp.dma_start(ks[b][r * E:(r + 1) * E, :, :],
                                     part[i][HD:2 * HD, :]).then_inc(s_stk[b], 16)

            stacks(0)
            sp.wait_ge(s_proj, 3)
            for k in range(2):
                sp.dma_start(xt[k], xT[:, :, (2 + k) * TB:(3 + k) * TB].rearrange("c p n -> p c n"))\
                  .then_inc(s_xt[k], 16)
            sp.dma_start(x1[:, 0:8, :], x[0:8].rearrange("t p n -> p t n")).then_inc(s_x[0], 16)
            sp.dma_start(gs_s[:], gs).then_inc(s_sc, 16)
            sp.dma_start(us_s[:], us).then_inc(s_sc, 16)
            sp.dma_start(sdr[:], ds).then_inc(s_sdr, 16)
            stacks(1)

            def max_rows(u, g):
                f = u * NG + g
                sp.wait_ge(s_mrow, f + 1)
                sp.wait_ge(s_mxf, (f + 1) * HG * BT * 2)
                b, k = divmod(u, N // TB)
                for i in range(3):
                    dst = qs[b][MROW + i:MROW + i + 1, k, g * HG:(g + 1) * HG, :]
                    sp.dma_start(dst, mp[:, f % 2, i, :]).then_inc(s_mld[g], 16)

            max_rows(0, 0)
            sp.wait_ge(s_stk[1], 16 * 27)
            sp.wait_ge(s_vt, B)
            sp.dma_start(x1[:, 8:16, :], x[8:16].rearrange("t p n -> p t n")).then_inc(s_x[1], 16)
            for u in range(NB):
                max_rows(u, 1)
                if u + 1 < NB:
                    max_rows(u + 1, 0)
            for blk in range(NB):
                sp.wait_ge(s_res, blk + 1)
                sp.dma_start(out[blk * BT:(blk + 1) * BT].rearrange("t p n -> p t n"),
                             x1[:, blk * BT:(blk + 1) * BT, :]).then_inc(s_out, 16)
            sp.wait_ge(s_out, 16 * NB)

        @block.gpsimd
        def _(pool):
            nc.gpsimd.memset(ident[:], 0.0).then_inc(s_id, 1)
            pool.wait_ge(s_id, 1)
            nc.gpsimd.affine_select(out=ident[:], in_=ident[:], compare_op=ALU.not_equal, fill=1.0, base=0,
                                    pattern=[[-1, P]], channel_multiplier=1).then_inc(s_id, 1)
            pool.wait_ge(s_id, 2)
            for b in range(B):
                for k, value in enumerate((ONES2, 0.0)):
                    if 2 * b + k:
                        pool.wait_ge(s_fill, 2 * b + k)
                    nc.gpsimd.memset(stack[b][64:96, k, :].bitcast(F32), value).then_inc(s_fill, 1)
            pool.wait_ge(s_parts, 3)
            pool.dma_start(wg[:], gq.rearrange("c p n -> p c n")).then_inc(s_gu, 16)
            pool.dma_start(wu[:], uq.rearrange("c p n -> p c n")).then_inc(s_gu, 16)
            pool.wait_ge(s_sds, 1)
            pool.dma_start(ds_scaled, sds[:]).then_inc(s_sdd, 16)
            pool.wait_ge(s_sdd, 16)

            def load_down(g):
                if g >= 2:
                    pool.wait_ge(s_w32, g - 1)
                pool.dma_start(dqs[:, g % 2, :], dq[g]).then_inc(s_dq[g % 2], 16)
                pool.dma_start(dsb[:, g % 2, :], ds_scaled[g:g + 1, :].to_broadcast([P, D])).then_inc(s_dsb[g % 2], 16)

            load_down(0)
            for g in range(G):
                if g + 1 < G:
                    load_down(g + 1)
                pool.wait_ge(s_dq[g % 2], 16 * (g // 2 + 1))
                pool.wait_ge(s_dsb[g % 2], 16 * (g // 2 + 1))
                if g:
                    pool.wait_ge(s_wl, g)
                else:
                    pool.wait_ge(s_fill, 4)
                nc.gpsimd.tensor_tensor(w32[:], dqs[:, g % 2, :], dsb[:, g % 2, :], ALU.mult).then_inc(s_w32, 1)
                if g == 0:
                    pool.wait_ge(s_scf, 2 * (NB // B) * STEPS)
                pool.wait_ge(s_w32, g + 1)
                nc.gpsimd.tensor_copy(wd[:, 0, g, :], w32[:]).then_inc(s_wh, 1)
                pool.wait_ge(s_wh, g + 1)
                nc.gpsimd.tensor_tensor(wd[:, 1, g, :], w32[:], wd[:, 0, g, :], ALU.subtract).then_inc(s_wl, 1)
            for t in range(NB * G):
                pool.wait_ge(s_mh, t + 1)
                if t:
                    pool.wait_ge(s_ml, t)
                else:
                    pool.wait_ge(s_wl, G)
                if t >= NM:
                    pool.wait_ge(s_dn, t - NM + 1)
                nc.gpsimd.tensor_tensor(mparts[:, 1, t % NM, :], sg[t % 2], mparts[:, 0, t % NM, :],
                                        ALU.subtract).then_inc(s_ml, 1)

        @block.scalar
        def _(act):
            def project(b):
                for k in range(2):
                    act.wait_ge(s_proj, 3 * b + k + 1)
                    if b and k == 0:
                        act.wait_ge(s_parts, 3 * b)
                    nc.scalar.activation(qkf[:, k * TB:(k + 1) * TB], bank[k], ACT.Identity, bias=bqk_s[:])\
                      .then_inc(s_projr, 1)
                act.wait_ge(s_proj, 3 * b + 3)
                if b:
                    act.wait_ge(s_vt, b)
                nc.scalar.activation(vtmp, bank[2], ACT.Identity, bias=bv_s[:]).then_inc(s_projr, 1)

            def exps(u, s):
                n = u * STEPS + s
                for pair in range(2):
                    pi = 2 * n + pair
                    act.wait_ge(s_scf, pi + 1)
                    if n >= 2:
                        act.wait_ge(s_av, n - 1)
                    nc.scalar.activation(pbuf[:, pi % 4, :].rearrange("p (a n) -> p a n", a=2),
                                         ps[:, 2 * (pi % 2):2 * (pi % 2) + 2, :], ACT.Exp).then_inc(s_exp, 1)

            def av_out(u, g):
                f = u * NG + g
                act.wait_ge(s_av, (f + 1) * KT)
                if f >= 2:
                    act.wait_ge(s_mf, misc_count("avT", *divmod(f - 2, NG)))
                nc.scalar.activation(avt[:, f % 2, :], bank[AVB], ACT.Copy).then_inc(s_ave, 1)

            def att_out(u):
                act.wait_ge(s_mf, misc_count("attT", u, 0))
                nc.scalar.activation(attT[:], bank[MISC][0:KR, :], ACT.Copy).then_inc(s_mr, 1)

            def deviation(n):
                act.wait_ge(s_st, n + 1)
                if n:
                    act.wait_ge(s_rstd, n)
                nc.scalar.activation(sd[:], mv[:, :, 1], ACT.Sqrt, bias=eps[:]).then_inc(s_sd, 1)

            def x1_high(u, c):
                act.wait_ge(s_mf, misc_count("x1T", u, c))
                if u == 2:
                    act.wait_ge(s_av, 2 * STEPS)
                nc.scalar.activation(x1t[u][:, 0, c, :], bank[MISC], ACT.Copy).then_inc(s_hi, 1)

            act.wait_ge(s_w, 16 * 5)
            act.wait_ge(s_const, 1)
            project(0)
            project(1)
            for u in range(NB + 1):
                for s in range(STEPS):
                    if u < NB:
                        exps(u, s)
                    if u and s == 0:
                        av_out(u - 1, 1)
                    if u < NB and s == KT:
                        av_out(u, 0)
                    for kind, v, k in misc_at(u, s):
                        if kind == "attT":
                            att_out(v)
                        if kind == "x1T":
                            x1_high(v, k)
                    if u and s == 5 + BT:
                        deviation(u - 1)

            def silu(t):
                act.wait_ge(s_gud, 6 * t + 5)
                if t >= 2:
                    act.wait_ge(s_ml, t - 1)
                nc.scalar.activation(sg[t % 2], ag[t % 2], ACT.Silu).then_inc(s_silu, 1)

            def inner_high(t):
                act.wait_ge(s_mul, t + 1)
                if t >= NM:
                    act.wait_ge(s_dn, t - NM + 1)
                nc.scalar.activation(mparts[:, 0, t % NM, :], sg[t % 2], ACT.Copy).then_inc(s_mh, 1)

            act.wait_ge(s_sc, 32)
            act.wait_ge(s_av, NB * STEPS)
            for t in range(NB * G + 2):
                blk, i = divmod(t, G)
                if t < NB * G:
                    for n, (dst, scl, freed) in enumerate(((ag, gs_s, s_silu), (au, us_s, s_mul))):
                        act.wait_ge(s_guf, 8 * t + n + 1)
                        if t >= 2:
                            act.wait_ge(freed, t - 1)
                        nc.scalar.activation(dst[t % 2], bank[GUB + n], ACT.Copy, scale=scl[:, i, 0:1])\
                          .then_inc(s_a0, 1)
                if t >= 2:
                    inner_high(t - 2)
                if 1 <= t <= NB * G:
                    silu(t - 1)
                if blk >= 1 and i == 5:
                    deviation(NB + blk - 1)
            deviation(2 * NB - 1)

        @block.tensor
        def _(pe):
            def projections(b):
                def qk(k):
                    pe.wait_ge(s_xt[k], 16 * (b + 1))
                    if b:
                        pe.wait_ge(s_projr, 3 * b)
                    for c in range(C):
                        mm = nc.tensor.matmul(bank[k], wqk_s[:, c, :], xt[k][:, c, :], start=(c == 0), stop=(c == C - 1))
                    mm.then_inc(s_proj, 1)

                def v():
                    for c in range(C):
                        for k in range(2):
                            mm = nc.tensor.matmul(bank[2][k * HD:(k + 1) * HD, :], wv_s[:, c, :], xt[k][:, c, :],
                                                  start=(c == 0), stop=(c == C - 1))
                    mm.then_inc(s_proj, 1)

                def vt():
                    pe.wait_ge(s_projr, 3 * (b + 1))
                    if b:
                        pe.wait_ge(s_vc, 2 * b)
                    else:
                        pe.wait_ge(s_id, 2)
                    for t in range(BT):
                        mm = nc.tensor.transpose(bank[3][:, t * P:(t + 1) * P], vtmp[:, t * P:(t + 1) * P], ident[:])
                    mm.then_inc(s_vt, 1)

                return [lambda: qk(0), lambda: qk(1), v, vt]

            def first_pass(n):
                u, r = divmod(n, H * BT * 2)
                h, r = divmod(r, BT * 2)
                qt, half = divmod(r, 2)
                b, k = divmod(u, N // TB)
                if n % (2 * H * BT * 2) == 0:
                    pe.wait_ge(s_stk[b], 16 * 27)
                if n >= 2:
                    pe.wait_ge(s_mxr, n - 1)
                nc.tensor.matmul(bank[MAXB + n % 2], qs[b][:, k, h, qt * P:(qt + 1) * P],
                                 ks[b][:, h, half * TB:(half + 1) * TB], start=True, stop=True).then_inc(s_mxf, 1)

            def misc(kind, u, k):
                if misc_count(kind, u, k) > 1:
                    pe.wait_ge(s_mr, misc_count(kind, u, k) - 1)
                f = u * NG + k
                if kind == "M":
                    pe.wait_ge(s_mxc, f + 1)
                    mm = nc.tensor.transpose(bank[MISC][0:HG * BT, 0:P], mx[:, f % 2, :], ident[:])
                elif kind == "avT":
                    pe.wait_ge(s_ave, f + 1)
                    for t in range(BT):
                        mm = nc.tensor.transpose(bank[MISC][:, t * P:(t + 1) * P], avt[:, f % 2, t * P:(t + 1) * P],
                                                 ident[:])
                elif kind == "attT":
                    for t in range(BT):
                        mm = nc.tensor.transpose(bank[MISC][0:KR, t * P:(t + 1) * P], att[:, t, :], ident[:])
                elif kind == "wo":
                    mm = nc.tensor.matmul(bank[MISC], attT[:, k * P:(k + 1) * P], wo_s[:], start=True, stop=True)
                else:
                    pe.wait_ge(s_x1, u + 1)
                    for t in range(BT):
                        mm = nc.tensor.transpose(bank[MISC][:, t * P:(t + 1) * P],
                                                 x1[:, u * BT + t, k * P:(k + 1) * P], ident[:])
                mm.then_inc(s_mf, 1)

            def scores(u, s, pair):
                g, kt = divmod(s, KT)
                b, k = divmod(u, N // TB)
                pi = 2 * (u * STEPS + s) + pair
                if kt == 0 and pair == 0:
                    pe.wait_ge(s_mld[g], 16 * 3 * (u + 1))
                if pi >= 2:
                    pe.wait_ge(s_exp, pi - 1)
                for j in range(2):
                    h = g * HG + 2 * pair + j
                    mm = nc.tensor.matmul(bank[2 * (pi % 2) + j], ks[b][:, h, kt * P:(kt + 1) * P],
                                          qs[b][:, k, h, :], start=True, stop=True)
                mm.then_inc(s_scf, 1)

            def av(n):
                u, s = divmod(n, STEPS)
                g, kt = divmod(s, KT)
                b = u * TB // N
                pe.wait_ge(s_exp, 2 * n + 2)
                if n == 0:
                    pe.wait_ge(s_vc, 2 * B)
                if kt == 0 and n:
                    pe.wait_ge(s_ave, n // KT)
                for j in range(HG):
                    mm = nc.tensor.matmul(bank[AVB][j * VC:(j + 1) * VC, :], vst[b][:, kt, g * HG + j, :],
                                          pbuf[:, (2 * n + j // 2) % 4, (j % 2) * TB:(j % 2 + 1) * TB],
                                          start=(kt == 0), stop=(kt == KT - 1))
                mm.then_inc(s_av, 1)

            pe.wait_ge(s_w, 16 * 5)
            for piece in projections(0):
                piece()
            later = projections(1)
            for s in range(STEPS):
                for j in range(4):
                    first_pass(4 * s + j)
                if s % 3 == 2 and s < 12:
                    later[s // 3]()
                if s == 9:
                    misc("M", 0, 0)
            for u in range(NB + 1):
                for s in range(STEPS):
                    n = u * STEPS + s
                    if u < NB:
                        for pair in range(2):
                            scores(u, s, pair)
                            if u + 1 < NB:
                                for j in range(2):
                                    first_pass(4 * (n + STEPS) + 2 * pair + j)
                    if 0 < n <= NB * STEPS:
                        av(n - 1)
                    for use in misc_at(u, s):
                        misc(*use)

            def down(t):
                blk, i = divmod(t, G)
                pe.wait_ge(s_ml, t + 1)
                if t == 0:
                    pe.wait_ge(s_wl, G)
                if i == 0 and blk:
                    pe.wait_ge(s_y, BT * blk)
                for k in range(BT):
                    for n, (a, w) in enumerate(((0, 0), (0, 1), (1, 0))):
                        mm = nc.tensor.matmul(bank[k], mparts[:, a, t % NM, k * P:(k + 1) * P], wd[:, w, i, :],
                                              start=(i == 0 and n == 0), stop=(i == G - 1 and n == 2))
                mm.then_inc(s_dn, 1)

            pe.wait_ge(s_mr, len(misc_order))
            pe.wait_ge(s_gu, 32)
            for t in range(NB * G + 2):
                blk, i = divmod(t, G)
                if t < NB * G:
                    for j in range(8):
                        c, n = divmod(j, 2)
                        w = (wg, wu)[n]
                        if j < 4:
                            if t:
                                pe.wait_ge(s_gud, 6 * (t - 1) + j + 3)
                        elif j < 6:
                            pe.wait_ge(s_a0, 2 * t + j - 3)
                        else:
                            pe.wait_ge(s_gud, 6 * t + j - 5)
                        for a in range(2):
                            mm = nc.tensor.matmul(bank[GUB + j % 4], w[:, c, i * P:(i + 1) * P], x1t[blk][:, a, c, :],
                                                  start=(a == 0), stop=(a == 1))
                        mm.then_inc(s_guf, 1)
                if t >= 2:
                    down(t - 2)

        @block.vector
        def _(dve):
            nc.vector.memset(eps[:], EPS).then_inc(s_const, 1)
            nc.vector.memset(att[:], 0.0).then_inc(s_zero, 1)
            nc.vector.memset(arena[:, 2:4, :], 0.0).then_inc(s_zero, 1)
            dve.wait_ge(s_zero, 2)
            nc.vector.memset(att[:, :, HD:HD + 1], 1.0)
            for b in range(B):
                nc.vector.memset(vst[b][:, :, :, E:E + 1], float(HD) ** 0.5)

            def split(b):
                dve.wait_ge(s_projr, 3 * b + 2)
                if b:
                    dve.wait_ge(s_stk[b - 1], 16 * 27)
                nc.vector.tensor_copy(part[0], qkf).then_inc(s_parts, 1)
                dve.wait_ge(s_parts, 3 * b + 1)
                nc.vector.tensor_tensor(res1, qkf, part[0], ALU.subtract).then_inc(s_split, 1)
                dve.wait_ge(s_split, b + 1)
                nc.vector.tensor_copy(part[1], res1).then_inc(s_parts, 1)
                dve.wait_ge(s_parts, 3 * b + 2)
                nc.vector.tensor_tensor(part[2], res1, part[1], ALU.subtract).then_inc(s_parts, 1)

            def place_v(b):
                dve.wait_ge(s_vt, b + 1)
                for k in range(2):
                    src = bank[3].rearrange("p (t k h e) -> p t k h e", t=BT, k=2, h=H)[:, :, k, :, :]
                    nc.vector.tensor_copy(vst[b][:, k * BT:(k + 1) * BT, :, 0:E], src).then_inc(s_vc, 1)

            def reduce(n):
                f, r = divmod(n, HG * BT * 2)
                qh, half = divmod(r, 2)
                dve.wait_ge(s_mxf, n + 1)
                nc.vector.tensor_reduce(mxh[:, f % 2, qh, half:half + 1], bank[MAXB + n % 2], AX.X, ALU.max)\
                  .then_inc(s_mxr, 1)

            def combine(f):
                dve.wait_ge(s_mxr, (f + 1) * HG * BT * 2)
                if f >= 2:
                    dve.wait_ge(s_mf, misc_count("M", *divmod(f - 2, NG)))
                nc.vector.tensor_tensor(mx[:, f % 2, :], mxh[:, f % 2, :, 0], mxh[:, f % 2, :, 1], ALU.max)\
                  .then_inc(s_mxc, 1)

            def split_max(u, g):
                f = u * NG + g
                dve.wait_ge(s_mf, misc_count("M", u, g))
                nc.vector.tensor_scalar(negm[:], bank[MISC][0:HG * BT, 0:P], -1.0, None, ALU.mult).then_inc(s_mr, 1)
                dve.wait_ge(s_mr, misc_count("M", u, g))
                if f >= 2:
                    dve.wait_ge(s_mld[g], 16 * 3 * u)
                nc.vector.tensor_copy(mp[:, f % 2, 0, :], negm[:]).then_inc(s_msp, 1)
                dve.wait_ge(s_msp, 4 * f + 1)
                nc.vector.tensor_tensor(mres[:, 0, :], negm[:], mp[:, f % 2, 0, :], ALU.subtract).then_inc(s_msp, 1)
                dve.wait_ge(s_msp, 4 * f + 2)
                nc.vector.tensor_copy(mp[:, f % 2, 1, :], mres[:, 0, :]).then_inc(s_msp, 1)
                dve.wait_ge(s_msp, 4 * f + 3)
                nc.vector.tensor_tensor(mres[:, 1, :], mres[:, 0, :], mp[:, f % 2, 1, :], ALU.subtract)\
                  .then_inc(s_msp, 1)
                dve.wait_ge(s_msp, 4 * f + 4)
                nc.vector.tensor_copy(mp[:, f % 2, 2, :], mres[:, 1, :]).then_inc(s_mrow, 1)

            def normalise(u, g):
                f = u * NG + g
                dve.wait_ge(s_mf, misc_count("avT", u, g))
                src = bank[MISC].rearrange("p (t h v) -> p t h v", t=BT, h=HG)
                nc.vector.reciprocal(rec[:], src[:, :, :, E]).then_inc(s_rec, 1)
                dve.wait_ge(s_rec, f + 1)
                dst = att[:, :, g * HG * E:(g + 1) * HG * E].rearrange("p t (h e) -> p t h e", h=HG)
                nc.vector.tensor_tensor(dst, src[:, :, :, 0:E], rec[:].unsqueeze(3).to_broadcast([P, BT, HG, E]),
                                        ALU.mult).then_inc(s_mr, 1)

            def add_attention(u, t):
                dve.wait_ge(s_mf, misc_count("wo", u, t))
                if t == 0:
                    dve.wait_ge(s_x[u * TB // N], 16)
                x1_t = x1[:, u * BT + t, :]
                nc.vector.tensor_tensor(x1_t, bank[MISC], x1_t, ALU.add).then_inc(s_mr, 1)
                dve.wait_ge(s_mr, misc_count("wo", u, t))
                nc.vector.bn_stats(st[:, t, :], x1_t).then_inc(s_bn, 1)

            def mean_variance(n):
                dve.wait_ge(s_bn, BT * (n + 1))
                for t in range(BT):
                    op = nc.vector.bn_aggr(mv[:, t, :], st[:, t, :])
                op.then_inc(s_st, 1)

            def apply(n, done):
                blk = n % NB
                dve.wait_ge(s_sd, n + 1)
                nc.vector.reciprocal(rstd[:], sd[:]).then_inc(s_rstd, 1)
                dve.wait_ge(s_rstd, n + 1)
                for t in range(BT):
                    x1_t = x1[:, blk * BT + t, :]
                    op = nc.vector.tensor_scalar(x1_t, x1_t, mv[:, t, 0:1], rstd[:, t:t + 1], ALU.subtract, ALU.mult)
                op.then_inc(done, 1)

            def x1_low(u, c):
                dve.wait_ge(s_hi, u * C + c + 1)
                nc.vector.tensor_tensor(x1t[u][:, 1, c, :], bank[MISC], x1t[u][:, 0, c, :], ALU.subtract)\
                  .then_inc(s_mr, 1)

            split(0)
            place_v(0)
            for u in range(-1, NB + 1):
                for s in range(STEPS):
                    if u + 1 < NB:
                        for j in range(4):
                            reduce(4 * ((u + 1) * STEPS + s) + j)
                        if s % KT == KT - 1:
                            combine((u + 1) * NG + s // KT)
                    if u == -1:
                        if s == 7:
                            split(1)
                        if s == 9:
                            split_max(0, 0)
                        if s == 12:
                            place_v(1)
                        if s == 13:
                            dve.wait_ge(s_sdr, 16)
                            nc.vector.tensor_scalar(sds[:], sdr[:], WSCALE, None, ALU.mult).then_inc(s_sds, 1)
                        continue
                    for kind, v, k in misc_at(u, s):
                        if kind == "M":
                            split_max(v, k)
                        if kind == "avT":
                            normalise(v, k)
                        if kind == "wo":
                            add_attention(v, k)
                        if kind == "x1T":
                            x1_low(v, k)
                    if u and s == 4 + BT:
                        mean_variance(u - 1)
                    if u and s == 6 + BT:
                        apply(u - 1, s_x1)

            def product(t):
                dve.wait_ge(s_silu, t + 1)
                dve.wait_ge(s_gud, 6 * t + 6)
                nc.vector.tensor_tensor(sg[t % 2], sg[t % 2], au[t % 2], ALU.mult).then_inc(s_mul, 1)

            def add_down(blk, t):
                y = x1[:, blk * BT + t, :]
                nc.vector.scalar_tensor_tensor(out=y, in0=bank[t], scalar=1.0 / WSCALE, in1=y, op0=ALU.mult,
                                               op1=ALU.add).then_inc(s_y, 1)

            def stats(blk, t):
                dve.wait_ge(s_y, BT * blk + t + 1)
                nc.vector.bn_stats(st[:, t, :], x1[:, blk * BT + t, :]).then_inc(s_bn, 1)

            for t in range(NB * G + 2):
                blk, i = divmod(t, G)
                if t < NB * G:
                    for j in range(2, 8):
                        c, n = divmod(j, 2)
                        acc, scl = ((ag, gs_s), (au, us_s))[n]
                        dve.wait_ge(s_guf, 8 * t + j + 1)
                        if c == 1:
                            dve.wait_ge(s_a0, 2 * t + n + 1)
                        else:
                            dve.wait_ge(s_gud, 6 * t + j - 3)
                        nc.vector.scalar_tensor_tensor(out=acc[t % 2], in0=bank[GUB + j % 4], scalar=scl[:, i, c:c + 1],
                                                       in1=acc[t % 2], op0=ALU.mult, op1=ALU.add).then_inc(s_gud, 1)
                if blk and i == 2:
                    dve.wait_ge(s_dn, blk * G)
                    for k in range(BT):
                        add_down(blk - 1, k)
                if 1 <= t <= NB * G:
                    product(t - 1)
                if blk and i in (3, 4):
                    for k in range(2 * (i - 3), 2 * (i - 2)):
                        stats(blk - 1, k)
                if blk and i == 4:
                    mean_variance(NB + blk - 1)
                if blk and i == 6:
                    apply(NB + blk - 1, s_res)
            dve.wait_ge(s_dn, NB * G)
            for k in range(BT):
                add_down(NB - 1, k)
            for k in range(BT):
                stats(NB - 1, k)
            mean_variance(2 * NB - 1)
            apply(2 * NB - 1, s_res)


def kernel(L0_attn_x, L0_attn_Wqk_w, L0_attn_Wqk_b, L0_attn_Wv_w, L0_attn_Wv_b, L0_attn_Wo_w, L0_attn_Wo_b,
           L0_ffn_gate_q, L0_ffn_gate_s, L0_ffn_up_q, L0_ffn_up_s, L0_ffn_down_q, L0_ffn_down_s):
    import concourse.bacc as bacc
    from concourse.bass_utils import run_bass_kernel_spmd

    x = np.asarray(L0_attn_x).reshape(T, D)
    wqk, bqk = np.asarray(L0_attn_Wqk_w), np.asarray(L0_attn_Wqk_b)
    wqk = wqk.reshape(H, E, 2, D).transpose(2, 1, 0, 3).reshape(2 * HD, D)
    bqk = bqk.reshape(H, E, 2).transpose(2, 1, 0).reshape(2 * HD, 1)
    bv = np.asarray(L0_attn_Wv_b)
    wo = np.zeros((KR, D), np.float32)
    wo[0:HD] = np.asarray(L0_attn_Wo_w).T
    wo[HD] = np.asarray(L0_attn_Wo_b)
    arrays = {
        "x": x.reshape(T // P, P, D),
        "xT": x.T.reshape(C, P, T),
        "wqkT": wqk.T.reshape(C, P, 2 * HD).transpose(1, 0, 2),
        "bqk": bqk,
        "wvT": np.asarray(L0_attn_Wv_w).T.reshape(C, P, HD).transpose(1, 0, 2),
        "bv": np.concatenate([bv, bv]).reshape(2 * HD, 1),
        "woT": wo,
        "gq": np.asarray(L0_ffn_gate_q).T.reshape(C, P, I),
        "gs": np.asarray(L0_ffn_gate_s).reshape(G, P, C).transpose(1, 0, 2),
        "uq": np.asarray(L0_ffn_up_q).T.reshape(C, P, I),
        "us": np.asarray(L0_ffn_up_s).reshape(G, P, C).transpose(1, 0, 2),
        "dq": np.asarray(L0_ffn_down_q).T.reshape(G, P, D),
        "ds": np.asarray(L0_ffn_down_s).T,
    }
    arrays = {name: np.ascontiguousarray(a) for name, a in arrays.items()}
    nc = bacc.Bacc("TRN2", target_bir_lowering=False, num_devices=1)
    args = [nc.dram_tensor(name, a.shape, mybir.dt.from_np(a.dtype), kind="ExternalInput").ap()
            for name, a in arrays.items()]
    out = nc.dram_tensor("out", (T // P, P, D), F32, kind="ExternalOutput").ap()
    build(nc, *args, out)
    r = run_bass_kernel_spmd(nc, [arrays], core_ids=[0])
    return r.results[0]["out"].reshape(B, N, D)
```

```python
from contextlib import ExitStack

import numpy as np
import concourse.bass as bass
from concourse import mybir

ALU = mybir.AluOpType
ACT = mybir.ActivationFunctionType
F32 = mybir.dt.float32
F16 = mybir.dt.float16
BF16 = mybir.dt.bfloat16
I32 = mybir.dt.int32
AX = mybir.AxisListType

P = 128
B, N, D = 2, 1024, 512
T = B * N
H, E = 8, 8
HD = H * E
I = 1792
C = D // P
G = I // P
TB = 512
NB = T // TB
BT = TB // P
KT = N // P
SLOTS = 12
KR = SLOTS * E
MROW = 9 * E
VC = 32
HG = 4
NG = H // HG
STEPS = NG * KT
ALL = NB * STEPS
FG = HG * BT * 2
FIRST = NB * NG * FG
AHEAD = FG + 12
TILES = NB * G
LAG = 6
NM = LAG + 2
EPS = 1e-5
WSCALE = 1024.0
MINUS_ONES = float(np.array([0xBF80BF80], np.uint32).view(np.float32)[0])


def build(nc, x, xT, wqkT, bqk, wvT, bv, woT, gq, gs, uq, us, dq, ds, out):
    ctx = ExitStack()
    with ctx:
        def sb(name, shape, dt):
            return ctx.enter_context(nc.sbuf_tensor(name, shape, dt))

        def sem(name):
            return ctx.enter_context(nc.semaphore(name))

        stack = [sb(f"stack{b}", [P, 2, H * N], BF16) for b in range(B)]
        ks = [stack[b][0:KR, 0, :].rearrange("p (h n) -> p h n", h=H) for b in range(B)]
        qs = [stack[b][0:KR, 1, :].rearrange("p (k h n) -> p k h n", k=N // TB, h=H) for b in range(B)]
        wd = stack[0][:, :, 0:G * D].bitcast(F16).rearrange("p s (g n) -> p s g n", g=G)
        mparts = stack[1][:, 0, 0:2 * NM * TB].bitcast(F16).rearrange("p (s k n) -> p s k n", s=2, k=NM)
        yt = stack[1][:, 1, 0:2 * BT * TB].bitcast(F32).rearrange("p (t n) -> p t n", t=BT)
        arena = sb("arena", [P, NB, C * TB], F32)
        xt = [arena[:, k, :].rearrange("p (c n) -> p c n", c=C) for k in range(2)]
        vst = [arena[:, 2 + b, :].rearrange("p (k h v) -> p k h v", k=KT, h=H) for b in range(B)]
        x1t = [arena[:, k, :].bitcast(F16).rearrange("p (s c n) -> p s c n", s=2, c=C) for k in range(NB)]
        x1 = sb("x1", [P, T // P, D], F32)
        qkf = x1[:, 8:10, :].rearrange("p a n -> p (a n)")
        res1 = x1[:, 10:12, :].rearrange("p a n -> p (a n)")
        part = [x1[:, 12 + i, :].bitcast(BF16) for i in range(3)]
        vtmp = x1[:, 15, :]
        wg = sb("wg", [P, C, I], F16)
        wu = sb("wu", [P, C, I], F16)
        pbuf = sb("pbuf", [P, 4, 2 * TB], F32)
        tmp = pbuf[:, :, :].rearrange("p a (b n) -> p (a b) n", b=2)
        ag, au, sg = [tmp[:, 0 + k, :] for k in range(2)], [tmp[:, 2 + k, :] for k in range(2)], \
            [tmp[:, 4 + k, :] for k in range(2)]
        dqs = sb("dqs", [P, 2, D], F16)
        dsb = sb("dsb", [P, 2, D], F32)
        w32 = sb("w32", [P, D], F32)
        sdr = sb("sdr", [G, D], F32)
        sds = sb("sds", [G, D], F32)
        wqk_s = sb("wqk_s", [P, C, 2 * HD], F32)
        wv_s = sb("wv_s", [P, C, HD], F32)
        wo_s = sb("wo_s", [KR, D], F32)
        bqk_s = sb("bqk_s", [P, 1], F32)
        bv_s = sb("bv_s", [P, 1], F32)
        gs_s = sb("gs_s", [P, G, C], F32)
        us_s = sb("us_s", [P, G, C], F32)
        ident = sb("ident", [P, P], F32)
        eps = sb("eps", [P, 1], F32)
        avt = sb("avt", [P, 2, TB], F32)
        att = sb("att", [P, BT, KR], F32)
        attT = sb("attT", [KR, TB], F32)
        rec = sb("rec", [P, BT, HG], F32)
        mxh = sb("mxh", [P, 2, HG * BT, 2], F32)
        mx = sb("mx", [P, 2, HG * BT], F32)
        mres = sb("mres", [HG * BT, 2, P], F32)
        mp = sb("mp", [HG * BT, 2, 3, P], BF16)
        st = sb("st", [P, BT, 6], F32)
        mv = sb("mv", [P, BT, 2], F32)
        sd = sb("sd", [P, BT], F32)
        rstd = sb("rstd", [P, BT], F32)

        ps = ctx.enter_context(nc.psum_tensor("ps", [P, 8, TB], F32))
        bank = [ps[:, k, :] for k in range(8)]
        MAXB, AVB, MISC, GUB = 4, 6, 7, 4
        ds_scaled = nc.dram_tensor("ds_scaled", [G, D], F32, kind="Internal").ap()

        s_xt = [[sem(f"xt_loaded{k}_{c}") for c in range(C)] for k in range(2)]
        s_wqk = sem("qk_weights_loaded")
        s_wv = sem("v_weights_loaded")
        s_wo = sem("out_weights_loaded")
        s_x = [sem(f"x_loaded{b}") for b in range(B)]
        s_gu = sem("gate_up_loaded")
        s_sc = sem("gate_up_scales_loaded")
        s_sdr = sem("down_scales_loaded")
        s_sds = sem("down_scales_multiplied")
        s_sdd = sem("down_scales_stored")
        s_dq = [sem(f"down_q_loaded{k}") for k in range(2)]
        s_dsb = [sem(f"down_scales_spread{k}") for k in range(2)]
        s_id = sem("identity_ready")
        s_fill = sem("stack_rows_filled")
        s_zero = sem("v_zeroed")
        s_const = sem("constants_set")
        s_proj = sem("projection_full")
        s_projr = sem("projection_read")
        s_vt = sem("v_transposed")
        s_vc = sem("v_placed")
        s_split = sem("qk_residual_ready")
        s_parts = sem("qk_parts_ready")
        s_stk = [sem(f"k_and_q_block0_stacked{b}") for b in range(B)]
        s_stq = [sem(f"q_block1_stacked{b}") for b in range(B)]
        s_mxf = sem("max_scores_full")
        s_mxr = sem("max_scores_read")
        s_mxc = sem("maxima_combined")
        s_msp = sem("maxima_split")
        s_mrow = sem("max_parts_ready")
        s_mld = [sem(f"max_rows_in_stack{g}") for g in range(NG)]
        s_scf = sem("scores_full")
        s_exp = sem("exp_done")
        s_av = sem("av_step_done")
        s_ave = sem("av_evacuated")
        s_mf = sem("misc_full")
        s_mr = sem("misc_read")
        s_rec = sem("denominators_inverted")
        s_bn = sem("ln_stats_of_tile")
        s_st = sem("ln_mean_variance_ready")
        s_sd = sem("ln_deviation_ready")
        s_rstd = sem("ln_inverse_ready")
        s_x1 = sem("x1_ready")
        s_hi = sem("x1t_high_ready")
        s_w32 = sem("down_weights_dequantised")
        s_wh = sem("down_weights_high_ready")
        s_wl = sem("down_weights_low_ready")
        s_guf = sem("gate_up_full")
        s_a0 = sem("first_group_scaled")
        s_gud = sem("group_added")
        s_silu = sem("silu_done")
        s_mul = sem("inner_ready")
        s_mh = sem("inner_high_ready")
        s_ml = sem("inner_low_ready")
        s_dn = sem("down_tile_done")
        s_dnl = sem("down_last_bank_done")
        s_ye = sem("down_evacuated")
        s_y = sem("down_added")
        s_res = sem("result_ready")
        s_out = sem("output_stored")

        block = ctx.enter_context(nc.Block())

        def misc_at(n):
            uses = []
            if n < ALL and (n + 3) % KT == 0:
                uses.append(("M", (n + 3) // KT, 0))
            f, r = divmod(n - 9, KT)
            if r == 0 and 0 <= f and n < ALL:
                uses.append(("avT", f, 0))
            u, r = divmod(n - STEPS, STEPS)
            if 0 <= u < NB - 1:
                if r == 2:
                    uses.append(("attT", u, 0))
                if 4 <= r < 4 + BT:
                    uses.append(("wo", u, r - 4))
                if 11 <= r < 11 + C:
                    uses.append(("x1T", u, r - 11))
            return [use for use in uses if use[0] != "M" or use[1] < NB * NG]

        tail = [("avT", NB * NG - 1, 0), ("attT", NB - 1, 0)] + [("wo", NB - 1, k) for k in range(BT)] \
            + [None, None] + [("x1T", NB - 1, c) for c in range(C)]

        def tail_at(t, half):
            i = 2 * t + half
            return [tail[i]] if i < len(tail) and tail[i] else []

        misc_order = [("M", 0, 0)] + [use for n in range(ALL) for use in misc_at(n)] + [use for use in tail if use]

        def misc_bank(*use):
            return bank[0] if use in tail else bank[MISC]

        def misc_count(*use):
            return misc_order.index(use) + 1

        @block.sync
        def _(sp):
            def load_xt(b):
                for k in range(2):
                    if b == 0 and k == 0:
                        sp.dma_start(wqk_s[:], wqkT).then_inc(s_wqk, 16)
                    for c in range(C):
                        q0 = (2 * b + k) * TB
                        sp.dma_start(xt[k][:, c, :], xT[c, :, q0:q0 + TB]).then_inc(s_xt[k][c], 16)
                    if b == 0 and k == 0:
                        sp.dma_start(bqk_s[:], bqk).then_inc(s_wqk, 16)

            def to_slots(b, i, block):
                for j in range(3):
                    if block == 0:
                        r = 3 * j + i
                        sp.dma_start(ks[b][r * E:(r + 1) * E, :, :], part[i][HD:2 * HD, :]).then_inc(s_stk[b], 16)
                    r = 3 * i + j
                    sp.dma_start(qs[b][r * E:(r + 1) * E, block, :, :],
                                 part[i][0:HD, block * TB:(block + 1) * TB]).then_inc((s_stk, s_stq)[block][b], 16)

            def stacks(b):
                sp.wait_ge(s_fill, 4)
                for i in range(3):
                    sp.wait_ge(s_parts, 3 * b + i + 1)
                    to_slots(b, i, 0)

            load_xt(0)
            sp.dma_start(wv_s[:], wvT).then_inc(s_wv, 16)
            sp.dma_start(bv_s[:], bv).then_inc(s_wv, 16)
            stacks(0)
            sp.wait_ge(s_proj, 3)
            load_xt(1)
            for i in range(3):
                to_slots(0, i, 1)
            sp.dma_start(wo_s[:], woT).then_inc(s_wo, 16)

            def max_rows(f):
                u, g = divmod(f, NG)
                sp.wait_ge(s_mrow, f + 1)
                sp.wait_ge(s_mxf, (f + 1) * FG)
                b, k = divmod(u, N // TB)
                for i in range(3):
                    dst = qs[b][MROW + i:MROW + i + 1, k, g * HG:(g + 1) * HG, :]
                    sp.dma_start(dst, mp[:, f % 2, i, :]).then_inc(s_mld[g], 16)

            max_rows(0)
            stacks(1)
            for i in range(3):
                to_slots(1, i, 1)
            sp.dma_start(x1[:, 0:8, :], x[0:8].rearrange("t p n -> p t n")).then_inc(s_x[0], 16)
            sp.dma_start(gs_s[:], gs).then_inc(s_sc, 16)
            sp.dma_start(us_s[:], us).then_inc(s_sc, 16)
            sp.dma_start(sdr[:], ds).then_inc(s_sdr, 16)
            max_rows(1)
            sp.wait_ge(s_stk[1], 16 * 18)
            sp.wait_ge(s_stq[1], 16 * 9)
            sp.wait_ge(s_vt, B)
            sp.dma_start(x1[:, 8:16, :], x[8:16].rearrange("t p n -> p t n")).then_inc(s_x[1], 16)
            for f in range(2, NB * NG):
                max_rows(f)
            for blk in range(NB - 1):
                sp.wait_ge(s_res, BT * (blk + 1))
                sp.dma_start(out[blk * BT:(blk + 1) * BT].rearrange("t p n -> p t n"),
                             x1[:, blk * BT:(blk + 1) * BT, :]).then_inc(s_out, 16)
            for t in range(T // P - BT, T // P):
                sp.wait_ge(s_res, t + 1)
                sp.dma_start(out[t], x1[:, t, :]).then_inc(s_out, 16)
            sp.wait_ge(s_out, 16 * (NB - 1 + BT))

        @block.gpsimd
        def _(pool):
            nc.gpsimd.memset(ident[:], 0.0).then_inc(s_id, 1)
            pool.wait_ge(s_id, 1)
            nc.gpsimd.affine_select(out=ident[:], in_=ident[:], compare_op=ALU.not_equal, fill=1.0, base=0,
                                    pattern=[[-1, P]], channel_multiplier=1).then_inc(s_id, 1)
            pool.wait_ge(s_id, 2)
            for b in range(B):
                for k, value in enumerate((MINUS_ONES, 0.0)):
                    if 2 * b + k:
                        pool.wait_ge(s_fill, 2 * b + k)
                    nc.gpsimd.memset(stack[b][64:96, k, :].bitcast(F32), value).then_inc(s_fill, 1)
            def load_down(g):
                if g >= 2:
                    pool.wait_ge(s_w32, g - 1)
                pool.dma_start(dqs[:, g % 2, :], dq[g]).then_inc(s_dq[g % 2], 16)
                pool.dma_start(dsb[:, g % 2, :], ds_scaled[g:g + 1, :].to_broadcast([P, D])).then_inc(s_dsb[g % 2], 16)

            def down_weights(g):
                if g + 1 < G:
                    load_down(g + 1)
                pool.wait_ge(s_dq[g % 2], 16 * (g // 2 + 1))
                pool.wait_ge(s_dsb[g % 2], 16 * (g // 2 + 1))
                if g:
                    pool.wait_ge(s_wl, g)
                else:
                    pool.wait_ge(s_fill, 4)
                nc.gpsimd.tensor_tensor(w32[:], dqs[:, g % 2, :], dsb[:, g % 2, :], ALU.mult).then_inc(s_w32, 1)
                if g == 0:
                    pool.wait_ge(s_scf, 2 * ALL // B)
                pool.wait_ge(s_w32, g + 1)
                nc.gpsimd.tensor_copy(wd[:, 0, g, :], w32[:]).then_inc(s_wh, 1)
                pool.wait_ge(s_wh, g + 1)
                nc.gpsimd.tensor_tensor(wd[:, 1, g, :], w32[:], wd[:, 0, g, :], ALU.subtract).then_inc(s_wl, 1)
                pool.wait_ge(s_wl, g + 1)

            pool.wait_ge(s_stk[0], 16 * 18)
            for c in range(C):
                pool.dma_start(wg[:, c, :], gq[c]).then_inc(s_gu, 16)
                pool.dma_start(wu[:, c, :], uq[c]).then_inc(s_gu, 16)
            pool.wait_ge(s_sds, 1)
            pool.dma_start(ds_scaled, sds[:]).then_inc(s_sdd, 16)
            pool.wait_ge(s_sdd, 16)
            load_down(0)
            for g in range(G):
                down_weights(g)

            def inner_low(t):
                pool.wait_ge(s_mh, t + 1)
                if t:
                    pool.wait_ge(s_ml, t)
                if t >= NM:
                    pool.wait_ge(s_dn, t - NM + 1)
                nc.gpsimd.tensor_tensor(mparts[:, 1, t % NM, :], sg[t % 2], mparts[:, 0, t % NM, :],
                                        ALU.subtract).then_inc(s_ml, 1)

            for t in range(TILES):
                inner_low(t)
                blk, i = divmod(t, G)
                if blk and LAG - 1 <= i < LAG - 1 + BT:
                    k = i - LAG + 1
                    n = BT * (blk - 1) + k
                    pool.wait_ge(s_ml, t + 1)
                    pool.wait_ge(s_ye, n + 1)
                    nc.gpsimd.tensor_tensor(x1[:, n, :], yt[:, k, :], x1[:, n, :], ALU.add).then_inc(s_y, 1)
                    pool.wait_ge(s_y, n + 1)

        @block.scalar
        def _(act):
            def project(b):
                for k in range(2):
                    act.wait_ge(s_proj, 3 * b + k + 1)
                    if b and k == 0:
                        act.wait_ge(s_parts, 3 * b)
                    nc.scalar.activation(qkf[:, k * TB:(k + 1) * TB], bank[k], ACT.Identity, bias=bqk_s[:])\
                      .then_inc(s_projr, 1)
                act.wait_ge(s_proj, 3 * b + 3)
                if b:
                    act.wait_ge(s_vt, b)
                nc.scalar.activation(vtmp, bank[2], ACT.Identity, bias=bv_s[:]).then_inc(s_projr, 1)

            def exps(n):
                for pair in range(2):
                    pi = 2 * n + pair
                    act.wait_ge(s_scf, pi + 1)
                    if n >= 2:
                        act.wait_ge(s_av, n - 1)
                    nc.scalar.activation(pbuf[:, pi % 4, :].rearrange("p (a n) -> p a n", a=2),
                                         ps[:, 2 * (pi % 2):2 * (pi % 2) + 2, :], ACT.Exp).then_inc(s_exp, 1)

            def av_out(f):
                act.wait_ge(s_av, (f + 1) * KT)
                if f >= 2:
                    act.wait_ge(s_mf, misc_count("avT", f - 2, 0))
                nc.scalar.activation(avt[:, f % 2, :], bank[AVB], ACT.Copy).then_inc(s_ave, 1)

            def att_out(u):
                act.wait_ge(s_mf, misc_count("attT", u, 0))
                nc.scalar.activation(attT[:], misc_bank("attT", u, 0)[0:KR, :], ACT.Copy).then_inc(s_mr, 1)

            def deviation(n):
                act.wait_ge(s_st, n + 1)
                if n:
                    act.wait_ge(s_rstd, n)
                nc.scalar.activation(sd[:], mv[:, :, 1], ACT.Sqrt, bias=eps[:]).then_inc(s_sd, 1)

            def x1_high(u, c):
                act.wait_ge(s_mf, misc_count("x1T", u, c))
                if u == 2:
                    act.wait_ge(s_av, 2 * STEPS)
                nc.scalar.activation(x1t[u][:, 0, c, :], misc_bank("x1T", u, c), ACT.Copy).then_inc(s_hi, 1)

            def misc_out(kind, u, k):
                if kind == "attT":
                    att_out(u)
                if kind == "x1T":
                    x1_high(u, k)

            act.wait_ge(s_wqk, 32)
            act.wait_ge(s_wv, 32)
            act.wait_ge(s_const, 1)
            project(0)
            project(1)
            for n in range(ALL):
                exps(n)
                if n and n % KT == 0:
                    av_out(n // KT - 1)
                for use in misc_at(n):
                    misc_out(*use)
                if n > STEPS and n % STEPS == 9:
                    deviation(n // STEPS - 1)
            av_out(NB * NG - 1)

            def silu(t):
                act.wait_ge(s_gud, 6 * t + 5)
                if t >= 2:
                    act.wait_ge(s_ml, t - 1)
                nc.scalar.activation(sg[t % 2], ag[t % 2], ACT.Silu).then_inc(s_silu, 1)

            def inner_high(t):
                act.wait_ge(s_mul, t + 1)
                if t >= NM:
                    act.wait_ge(s_dn, t - NM + 1)
                nc.scalar.activation(mparts[:, 0, t % NM, :], sg[t % 2], ACT.Copy).then_inc(s_mh, 1)

            def down_out(k, blk):
                act.wait_ge(s_dn, G * (blk + 1))
                if blk:
                    act.wait_ge(s_y, BT * (blk - 1) + k + 1)
                nc.scalar.activation(yt[:, k, :], bank[k], ACT.Copy, scale=1.0 / WSCALE).then_inc(s_ye, 1)

            act.wait_ge(s_sc, 32)
            act.wait_ge(s_av, ALL)
            for t in range(TILES + 2):
                blk, i = divmod(t, G)
                if t < TILES:
                    for n, (dst, scl, freed) in enumerate(((ag, gs_s, s_silu), (au, us_s, s_mul))):
                        act.wait_ge(s_guf, 8 * t + n + 1)
                        if t >= 2:
                            act.wait_ge(freed, t - 1)
                        nc.scalar.activation(dst[t % 2], bank[GUB + n], ACT.Copy, scale=scl[:, i, 0:1])\
                          .then_inc(s_a0, 1)
                for use in tail_at(t, 0):
                    misc_out(*use)
                if t < TILES and blk and i == LAG:
                    for k in range(BT):
                        down_out(k, blk - 1)
                if t >= 2:
                    inner_high(t - 2)
                if 1 <= t <= TILES:
                    silu(t - 1)
                for use in tail_at(t, 1):
                    misc_out(*use)
                if t == 3:
                    deviation(NB - 1)
                if t < TILES and blk and i == G - 1:
                    deviation(NB + blk - 1)
            deviation(2 * NB - 1)

        @block.tensor
        def _(pe):
            def projections(b):
                def qk(k, c):
                    pe.wait_ge(s_xt[k][c], 16 * (b + 1))
                    if b and c == 0:
                        pe.wait_ge(s_projr, 3 * b)
                    mm = nc.tensor.matmul(bank[k], wqk_s[:, c, :], xt[k][:, c, :], start=(c == 0), stop=(c == C - 1))
                    if c == C - 1:
                        mm.then_inc(s_proj, 1)

                def v(c):
                    for k in range(2):
                        mm = nc.tensor.matmul(bank[2][k * HD:(k + 1) * HD, :], wv_s[:, c, :], xt[k][:, c, :],
                                              start=(c == 0), stop=(c == C - 1))
                    if c == C - 1:
                        mm.then_inc(s_proj, 1)

                def vt():
                    pe.wait_ge(s_projr, 3 * (b + 1))
                    if b:
                        pe.wait_ge(s_vc, 2 * b)
                    else:
                        pe.wait_ge(s_id, 2)
                    for t in range(BT):
                        mm = nc.tensor.transpose(bank[3][:, t * P:(t + 1) * P], vtmp[:, t * P:(t + 1) * P], ident[:])
                    mm.then_inc(s_vt, 1)

                return [(qk, k, c) for k in range(2) for c in range(C)] + [(v, c) for c in range(C)] + [(vt,)]

            def first_pass(n):
                u, r = divmod(n, H * BT * 2)
                h, r = divmod(r, BT * 2)
                qt, half = divmod(r, 2)
                b, k = divmod(u, N // TB)
                if n % (4 * FG) == 0:
                    pe.wait_ge(s_stk[b], 16 * 18)
                elif n % (2 * FG) == 0:
                    pe.wait_ge(s_stq[b], 16 * 9)
                if n >= 2:
                    pe.wait_ge(s_mxr, n - 1)
                nc.tensor.matmul(bank[MAXB + n % 2], qs[b][:, k, h, qt * P:(qt + 1) * P],
                                 ks[b][:, h, half * TB:(half + 1) * TB], start=True, stop=True).then_inc(s_mxf, 1)

            def misc(kind, u, k):
                if misc_count(kind, u, k) > 1:
                    pe.wait_ge(s_mr, misc_count(kind, u, k) - 1)
                if (kind, u, k) == tail[0]:
                    pe.wait_ge(s_exp, 2 * ALL)
                dst = misc_bank(kind, u, k)
                if kind == "M":
                    pe.wait_ge(s_mxc, u + 1)
                    mm = nc.tensor.transpose(dst[0:HG * BT, 0:P], mx[:, u % 2, :], ident[:])
                elif kind == "avT":
                    pe.wait_ge(s_ave, u + 1)
                    for t in range(BT):
                        mm = nc.tensor.transpose(dst[:, t * P:(t + 1) * P], avt[:, u % 2, t * P:(t + 1) * P], ident[:])
                elif kind == "attT":
                    for t in range(BT):
                        mm = nc.tensor.transpose(dst[0:KR, t * P:(t + 1) * P], att[:, t, :], ident[:])
                elif kind == "wo":
                    if k == 0:
                        pe.wait_ge(s_wo, 16)
                    mm = nc.tensor.matmul(dst, attT[:, k * P:(k + 1) * P], wo_s[:], start=True, stop=True)
                else:
                    pe.wait_ge(s_x1, u + 1)
                    for t in range(BT):
                        mm = nc.tensor.transpose(dst[:, t * P:(t + 1) * P], x1[:, u * BT + t, k * P:(k + 1) * P],
                                                 ident[:])
                mm.then_inc(s_mf, 1)

            def scores(n, pair):
                u, s = divmod(n, STEPS)
                g, kt = divmod(s, KT)
                b, k = divmod(u, N // TB)
                pi = 2 * n + pair
                if kt == 0 and pair == 0:
                    pe.wait_ge(s_mld[g], 16 * 3 * (u + 1))
                if pi >= 2:
                    pe.wait_ge(s_exp, pi - 1)
                elif pi == 0:
                    pe.wait_ge(s_vc, 2 * B)
                for j in range(2):
                    h = g * HG + 2 * pair + j
                    mm = nc.tensor.matmul(bank[2 * (pi % 2) + j], ks[b][:, h, kt * P:(kt + 1) * P],
                                          qs[b][:, k, h, :], start=True, stop=True)
                mm.then_inc(s_scf, 1)

            def av(n):
                u, s = divmod(n, STEPS)
                g, kt = divmod(s, KT)
                b = u * TB // N
                pe.wait_ge(s_exp, 2 * n + 2)
                if n == 0:
                    pe.wait_ge(s_vc, 2 * B)
                if kt == 0 and n:
                    pe.wait_ge(s_ave, n // KT)
                for j in range(HG):
                    mm = nc.tensor.matmul(bank[AVB][j * VC:(j + 1) * VC, :], vst[b][:, kt, g * HG + j, :],
                                          pbuf[:, (2 * n + j // 2) % 4, (j % 2) * TB:(j % 2 + 1) * TB],
                                          start=(kt == 0), stop=(kt == KT - 1))
                mm.then_inc(s_av, 1)

            def piece(p):
                p[0](*p[1:])

            pe.wait_ge(s_wqk, 32)
            for n, p in enumerate(projections(0)):
                if n == 2 * C:
                    pe.wait_ge(s_wv, 32)
                piece(p)
            later = projections(1)
            for n in range(AHEAD):
                first_pass(n)
                if n >= 8 and n % 2 and later:
                    piece(later.pop(0))
                if n == FG + 2:
                    misc("M", 0, 0)
            for n in range(ALL):
                ahead = [AHEAD + 4 * n + j for j in range(4) if AHEAD + 4 * n + j < FIRST]
                for pair in range(2):
                    scores(n, pair)
                    for m in ahead[pair:pair + 1]:
                        first_pass(m)
                    for use in misc_at(n):
                        if pair == 0 and use[0] == "M":
                            misc(*use)
                if n:
                    av(n - 1)
                for m in ahead[2:]:
                    first_pass(m)
                for use in misc_at(n):
                    if use[0] != "M":
                        misc(*use)
            av(ALL - 1)

            def down(t):
                blk, i = divmod(t, G)
                pe.wait_ge(s_ml, t + 1)
                if t == 0:
                    pe.wait_ge(s_wl, G)
                    pe.wait_ge(s_mr, len(misc_order))
                if i == 0 and blk:
                    pe.wait_ge(s_ye, BT * blk)
                for k in range(BT):
                    for n, (a, w) in enumerate(((0, 0), (0, 1), (1, 0))):
                        mm = nc.tensor.matmul(bank[k], mparts[:, a, t % NM, k * P:(k + 1) * P], wd[:, w, i, :],
                                              start=(i == 0 and n == 0), stop=(i == G - 1 and n == 2))
                    if t == TILES - 1:
                        mm.then_inc(s_dnl, 1)
                if t < TILES - 1:
                    mm.then_inc(s_dn, 1)

            pe.wait_ge(s_gu, 16 * 2 * C)
            pe.wait_ge(s_mxr, FIRST)
            pe.wait_ge(s_mr, len(misc_order) - len([use for use in tail if use]))
            for t in range(TILES + LAG):
                blk, i = divmod(t, G)
                if t < TILES:
                    for j in range(8):
                        c, n = divmod(j, 2)
                        w = (wg, wu)[n]
                        if j < 4:
                            if t:
                                pe.wait_ge(s_gud, 6 * (t - 1) + j + 3)
                            elif j == AVB - GUB:
                                pe.wait_ge(s_ave, NB * NG)
                        elif j < 6:
                            pe.wait_ge(s_a0, 2 * t + j - 3)
                        else:
                            pe.wait_ge(s_gud, 6 * t + j - 5)
                        for a in range(2):
                            mm = nc.tensor.matmul(bank[GUB + j % 4], w[:, c, i * P:(i + 1) * P], x1t[blk][:, a, c, :],
                                                  start=(a == 0), stop=(a == 1))
                        mm.then_inc(s_guf, 1)
                        if j in (2, 6):
                            for use in tail_at(t, j // 4):
                                misc(*use)
                if t >= LAG:
                    down(t - LAG)

        @block.vector
        def _(dve):
            nc.vector.memset(eps[:], EPS).then_inc(s_const, 1)
            nc.vector.memset(att[:], 0.0).then_inc(s_zero, 1)
            nc.vector.memset(arena[:, 2:4, :], 0.0).then_inc(s_zero, 1)
            dve.wait_ge(s_zero, 2)
            nc.vector.memset(att[:, :, HD:HD + 1], 1.0)
            for b in range(B):
                nc.vector.memset(vst[b][:, :, :, E:E + 1], float(HD) ** 0.5)

            def split(b):
                dve.wait_ge(s_projr, 3 * b + 2)
                if b:
                    dve.wait_ge(s_stk[b - 1], 16 * 18)
                    dve.wait_ge(s_stq[b - 1], 16 * 9)
                nc.vector.tensor_copy(part[0], qkf).then_inc(s_parts, 1)
                yield
                dve.wait_ge(s_parts, 3 * b + 1)
                nc.vector.tensor_tensor(res1, qkf, part[0], ALU.subtract).then_inc(s_split, 1)
                yield
                dve.wait_ge(s_split, b + 1)
                nc.vector.tensor_copy(part[1], res1).then_inc(s_parts, 1)
                yield
                dve.wait_ge(s_parts, 3 * b + 2)
                nc.vector.tensor_tensor(part[2], res1, part[1], ALU.subtract).then_inc(s_parts, 1)
                yield

            def place_v(b):
                dve.wait_ge(s_vt, b + 1)
                for k in range(2):
                    src = bank[3].rearrange("p (t k h e) -> p t k h e", t=BT, k=2, h=H)[:, :, k, :, :]
                    nc.vector.tensor_copy(vst[b][:, k * BT:(k + 1) * BT, :, 0:E], src).then_inc(s_vc, 1)

            def reduce(n):
                f, r = divmod(n, HG * BT * 2)
                qh, half = divmod(r, 2)
                dve.wait_ge(s_mxf, n + 1)
                nc.vector.tensor_reduce(mxh[:, f % 2, qh, half:half + 1], bank[MAXB + n % 2], AX.X, ALU.max)\
                  .then_inc(s_mxr, 1)

            def combine(f):
                dve.wait_ge(s_mxr, (f + 1) * HG * BT * 2)
                if f >= 2:
                    dve.wait_ge(s_mf, misc_count("M", f - 2, 0))
                nc.vector.tensor_tensor(mx[:, f % 2, :], mxh[:, f % 2, :, 0], mxh[:, f % 2, :, 1], ALU.max)\
                  .then_inc(s_mxc, 1)

            def split_max(f):
                dve.wait_ge(s_mf, misc_count("M", f, 0))
                if f >= 2:
                    dve.wait_ge(s_mld[f % NG], 16 * 3 * (f // NG))
                rows = bank[MISC][0:HG * BT, 0:P]
                nc.vector.tensor_copy(mp[:, f % 2, 0, :], rows).then_inc(s_msp, 1)
                dve.wait_ge(s_msp, 3 * f + 1)
                nc.vector.tensor_tensor(mres[:, 0, :], rows, mp[:, f % 2, 0, :], ALU.subtract).then_inc(s_mr, 1)
                dve.wait_ge(s_mr, misc_count("M", f, 0))
                nc.vector.tensor_copy(mp[:, f % 2, 1, :], mres[:, 0, :]).then_inc(s_msp, 1)
                dve.wait_ge(s_msp, 3 * f + 2)
                nc.vector.tensor_tensor(mres[:, 1, :], mres[:, 0, :], mp[:, f % 2, 1, :], ALU.subtract)\
                  .then_inc(s_msp, 1)
                dve.wait_ge(s_msp, 3 * f + 3)
                nc.vector.tensor_copy(mp[:, f % 2, 2, :], mres[:, 1, :]).then_inc(s_mrow, 1)

            def normalise(f):
                dve.wait_ge(s_mf, misc_count("avT", f, 0))
                g = f % NG
                src = misc_bank("avT", f, 0).rearrange("p (t h v) -> p t h v", t=BT, h=HG)
                nc.vector.reciprocal(rec[:], src[:, :, :, E]).then_inc(s_rec, 1)
                dve.wait_ge(s_rec, f + 1)
                dst = att[:, :, g * HG * E:(g + 1) * HG * E].rearrange("p t (h e) -> p t h e", h=HG)
                nc.vector.tensor_tensor(dst, src[:, :, :, 0:E], rec[:].unsqueeze(3).to_broadcast([P, BT, HG, E]),
                                        ALU.mult).then_inc(s_mr, 1)

            def add_attention(u, t):
                dve.wait_ge(s_mf, misc_count("wo", u, t))
                if t == 0:
                    dve.wait_ge(s_x[u * TB // N], 16)
                x1_t = x1[:, u * BT + t, :]
                nc.vector.tensor_tensor(x1_t, misc_bank("wo", u, t), x1_t, ALU.add).then_inc(s_mr, 1)
                dve.wait_ge(s_mr, misc_count("wo", u, t))
                nc.vector.bn_stats(st[:, t, :], x1_t).then_inc(s_bn, 1)

            def mean_variance(n):
                dve.wait_ge(s_bn, BT * (n + 1))
                for t in range(BT):
                    op = nc.vector.bn_aggr(mv[:, t, :], st[:, t, :])
                op.then_inc(s_st, 1)

            def apply(n, done):
                blk = n % NB
                dve.wait_ge(s_sd, n + 1)
                nc.vector.reciprocal(rstd[:], sd[:]).then_inc(s_rstd, 1)
                dve.wait_ge(s_rstd, n + 1)
                for t in range(BT):
                    x1_t = x1[:, blk * BT + t, :]
                    op = nc.vector.tensor_scalar(x1_t, x1_t, mv[:, t, 0:1], rstd[:, t:t + 1], ALU.subtract, ALU.mult)
                    if done is s_res:
                        op.then_inc(s_res, 1)
                if done is not s_res:
                    op.then_inc(done, 1)

            def x1_low(u, c):
                dve.wait_ge(s_hi, u * C + c + 1)
                nc.vector.tensor_tensor(x1t[u][:, 1, c, :], misc_bank("x1T", u, c), x1t[u][:, 0, c, :], ALU.subtract)\
                  .then_inc(s_mr, 1)

            for _ in split(0):
                pass
            place_v(0)
            def misc_read(kind, u, k):
                if kind == "M":
                    split_max(u)
                if kind == "avT":
                    normalise(u)
                if kind == "wo":
                    add_attention(u, k)
                if kind == "x1T":
                    x1_low(u, k)

            def maxima(n):
                reduce(n)
                if (n + 1) % FG == 0:
                    combine(n // FG)

            for n in range(AHEAD):
                maxima(n)
                if n == 28:
                    pieces = split(1)
                if n >= 28 and n % 2 == 0 and n < 36:
                    next(pieces)
                if n == FG + 4:
                    split_max(0)
                if n == AHEAD - 2:
                    place_v(1)
            for n in range(ALL):
                for j in range(4):
                    if AHEAD + 4 * n + j < FIRST:
                        maxima(AHEAD + 4 * n + j)
                if n == 4:
                    dve.wait_ge(s_sdr, 16)
                    nc.vector.tensor_scalar(sds[:], sdr[:], WSCALE, None, ALU.mult).then_inc(s_sds, 1)
                for use in misc_at(n):
                    misc_read(*use)
                if n > STEPS and n % STEPS == 8:
                    mean_variance(n // STEPS - 1)
                if n > STEPS and n % STEPS == 10:
                    apply(n // STEPS - 1, s_x1)

            def product(t):
                dve.wait_ge(s_silu, t + 1)
                dve.wait_ge(s_gud, 6 * t + 6)
                nc.vector.tensor_tensor(sg[t % 2], sg[t % 2], au[t % 2], ALU.mult).then_inc(s_mul, 1)

            def stats(blk, t):
                dve.wait_ge(s_y, BT * blk + t + 1)
                nc.vector.bn_stats(st[:, t, :], x1[:, blk * BT + t, :]).then_inc(s_bn, 1)

            for t in range(TILES + 1):
                blk, i = divmod(t, G)
                if t < TILES:
                    for j in range(2, 8):
                        c, n = divmod(j, 2)
                        acc, scl = ((ag, gs_s), (au, us_s))[n]
                        dve.wait_ge(s_guf, 8 * t + j + 1)
                        if c == 1:
                            dve.wait_ge(s_a0, 2 * t + n + 1)
                        else:
                            dve.wait_ge(s_gud, 6 * t + j - 3)
                        nc.vector.scalar_tensor_tensor(out=acc[t % 2], in0=bank[GUB + j % 4], scalar=scl[:, i, c:c + 1],
                                                       in1=acc[t % 2], op0=ALU.mult, op1=ALU.add).then_inc(s_gud, 1)
                        if j in (3, 7):
                            for use in tail_at(t, j // 4):
                                misc_read(*use)
                if 1 <= t <= TILES:
                    product(t - 1)
                if t == 2:
                    mean_variance(NB - 1)
                if t == 3:
                    apply(NB - 1, s_x1)
                if t < TILES and blk and LAG + 3 <= i < LAG + 3 + BT:
                    stats(blk - 1, i - LAG - 3)
                if t < TILES and blk and i == LAG + 2 + BT:
                    mean_variance(NB + blk - 1)
                if blk >= 2 and i == 0:
                    apply(NB + blk - 2, s_res)
            for k in range(BT):
                n = (NB - 1) * BT + k
                dve.wait_ge(s_dnl, k + 1)
                nc.vector.scalar_tensor_tensor(out=x1[:, n, :], in0=bank[k], scalar=1.0 / WSCALE, in1=x1[:, n, :],
                                               op0=ALU.mult, op1=ALU.add).then_inc(s_y, 1)
                stats(NB - 1, k)
            mean_variance(2 * NB - 1)
            apply(2 * NB - 1, s_res)


def kernel(L0_attn_x, L0_attn_Wqk_w, L0_attn_Wqk_b, L0_attn_Wv_w, L0_attn_Wv_b, L0_attn_Wo_w, L0_attn_Wo_b,
           L0_ffn_gate_q, L0_ffn_gate_s, L0_ffn_up_q, L0_ffn_up_s, L0_ffn_down_q, L0_ffn_down_s):
    import concourse.bacc as bacc
    from concourse.bass_utils import run_bass_kernel_spmd

    x = np.asarray(L0_attn_x).reshape(T, D)
    wqk, bqk = np.asarray(L0_attn_Wqk_w), np.asarray(L0_attn_Wqk_b)
    wqk = wqk.reshape(H, E, 2, D).transpose(2, 1, 0, 3).reshape(2 * HD, D)
    bqk = bqk.reshape(H, E, 2).transpose(2, 1, 0).reshape(2 * HD, 1)
    bv = np.asarray(L0_attn_Wv_b)
    wo = np.zeros((KR, D), np.float32)
    wo[0:HD] = np.asarray(L0_attn_Wo_w).T
    wo[HD] = np.asarray(L0_attn_Wo_b)
    arrays = {
        "x": x.reshape(T // P, P, D),
        "xT": x.T.reshape(C, P, T),
        "wqkT": wqk.T.reshape(C, P, 2 * HD).transpose(1, 0, 2),
        "bqk": bqk,
        "wvT": np.asarray(L0_attn_Wv_w).T.reshape(C, P, HD).transpose(1, 0, 2),
        "bv": np.concatenate([bv, bv]).reshape(2 * HD, 1),
        "woT": wo,
        "gq": np.asarray(L0_ffn_gate_q).T.reshape(C, P, I),
        "gs": np.asarray(L0_ffn_gate_s).reshape(G, P, C).transpose(1, 0, 2),
        "uq": np.asarray(L0_ffn_up_q).T.reshape(C, P, I),
        "us": np.asarray(L0_ffn_up_s).reshape(G, P, C).transpose(1, 0, 2),
        "dq": np.asarray(L0_ffn_down_q).T.reshape(G, P, D),
        "ds": np.asarray(L0_ffn_down_s).T,
    }
    arrays = {name: np.ascontiguousarray(a) for name, a in arrays.items()}
    nc = bacc.Bacc("TRN2", target_bir_lowering=False, num_devices=1)
    args = [nc.dram_tensor(name, a.shape, mybir.dt.from_np(a.dtype), kind="ExternalInput").ap()
            for name, a in arrays.items()]
    out = nc.dram_tensor("out", (T // P, P, D), F32, kind="ExternalOutput").ap()
    build(nc, *args, out)
    r = run_bass_kernel_spmd(nc, [arrays], core_ids=[0])
    return r.results[0]["out"].reshape(B, N, D)
```

```python
from contextlib import ExitStack

import numpy as np
import concourse.bass as bass
from concourse import mybir

ALU = mybir.AluOpType
ACT = mybir.ActivationFunctionType
F32 = mybir.dt.float32
F16 = mybir.dt.float16
BF16 = mybir.dt.bfloat16
AX = mybir.AxisListType

P = 128
B, N, D = 2, 1024, 512
T = B * N
H, E = 8, 8
HD = H * E
I = 1792
C = D // P
G = I // P
TB = 512
NB = T // TB
BT = TB // P
KT = N // P
SLOTS = 12
KR = SLOTS * E
MROW = 9 * E
VC = 32
HG = 4
NG = H // HG
STEPS = NG * KT
ALL = NB * STEPS
FG = HG * BT * 2
FIRST = NB * NG * FG
AHEAD = FG + 14
TILES = NB * G
LAG = 3
NM = LAG + 2
EPS = 1e-5
MINUS_ONES = float(np.array([0xBF80BF80], np.uint32).view(np.float32)[0])


def build(nc, x, xT, wqkT, bqk, wvT, bv, woT, gq, gs, uq, us, dq, ds, out):
    ctx = ExitStack()
    with ctx:
        def sb(name, shape, dt):
            return ctx.enter_context(nc.sbuf_tensor(name, shape, dt))

        def sem(name):
            return ctx.enter_context(nc.semaphore(name))

        stack = [sb(f"stack{b}", [P, 2, H * N], BF16) for b in range(B)]
        ks = [stack[b][0:KR, 0, :].rearrange("p (h n) -> p h n", h=H) for b in range(B)]
        qs = [stack[b][0:KR, 1, :].rearrange("p (k h n) -> p k h n", k=N // TB, h=H) for b in range(B)]
        wd = stack[0][:, 0, 0:G * D].bitcast(F16).rearrange("p (g n) -> p g n", g=G)
        yacc = stack[0][:, 1, :].bitcast(F32).rearrange("p (b c n) -> p b c n", b=2, c=C)
        mparts = stack[1][:, 0, 0:2 * NM * TB].bitcast(F16).rearrange("p (s k n) -> p s k n", s=2, k=NM)
        arena = sb("arena", [P, NB, C * TB], F32)
        xt = [arena[:, k, :].rearrange("p (c n) -> p c n", c=C) for k in range(2)]
        vst = [arena[:, 2 + b, :].rearrange("p (k h v) -> p k h v", k=KT, h=H) for b in range(B)]
        x1t = [arena[:, k, :].bitcast(F16).rearrange("p (s c n) -> p s c n", s=2, c=C) for k in range(NB)]
        x1 = sb("x1", [P, T // P, D], F32)
        qkf = x1[:, 8:10, :].rearrange("p a n -> p (a n)")
        res1 = x1[:, 10:12, :].rearrange("p a n -> p (a n)")
        part = [x1[:, 12 + i, :].bitcast(BF16) for i in range(3)]
        vtmp = x1[:, 15, :]
        wg = sb("wg", [P, C, I], F16)
        wu = sb("wu", [P, C, I], F16)
        pbuf = sb("pbuf", [P, 4, 2 * TB], F32)
        tmp = pbuf[:, :, :].rearrange("p a (b n) -> p (a b) n", b=2)
        ag, au, sg = [tmp[:, 0 + k, :] for k in range(2)], [tmp[:, 2 + k, :] for k in range(2)], \
            [tmp[:, 4 + k, :] for k in range(2)]
        b1 = sb("b1", [P, 2, TB], F32)
        bg, bu = [tmp[:, 6, :], b1[:, 0, :]], [tmp[:, 7, :], b1[:, 1, :]]
        yscaled = sb("yscaled", [P, 2, TB], F32)
        x32 = sb("x32", [P, C, D], F32)
        wqk_s = sb("wqk_s", [P, C, 2 * HD], F32)
        wv_s = sb("wv_s", [P, C, HD], F32)
        wo_s = sb("wo_s", [KR, D], F32)
        bqk_s = sb("bqk_s", [P, 1], F32)
        bv_s = sb("bv_s", [P, 1], F32)
        gs_s = sb("gs_s", [P, G, C], F32)
        us_s = sb("us_s", [P, G, C], F32)
        ds_s = sb("ds_s", [P, C, G], F32)
        ident = sb("ident", [P, P], F32)
        mhalf = sb("mhalf", [P, BT], F32)
        warm = sb("warm", [P, 1], F32)
        avt = sb("avt", [P, 2, TB], F32)
        att = sb("att", [P, BT, KR], F32)
        attT = sb("attT", [KR, TB], F32)
        rec = sb("rec", [P, BT, HG], F32)
        mxh = sb("mxh", [P, 2, HG * BT, 2], F32)
        mx = sb("mx", [P, 2, HG * BT], F32)
        mres = sb("mres", [HG * BT, 2, P], F32)
        mp = sb("mp", [HG * BT, 2, 3, P], BF16)
        st = sb("st", [P, BT, 6], F32)
        mv = sb("mv", [P, BT, 2], F32)
        veps = sb("veps", [P, BT], F32)
        rstd = sb("rstd", [P, BT], F32)

        ps = ctx.enter_context(nc.psum_tensor("ps", [P, 8, TB], F32))
        bank = [ps[:, k, :] for k in range(8)]
        AVB, GUB = 6, 4
        RING = (4, 5, 7)

        s_xt = [[sem(f"xt_loaded{k}_{c}") for c in range(C)] for k in range(2)]
        s_wqk = sem("qk_weights_loaded")
        s_bqk = sem("qk_bias_loaded")
        s_wv = sem("v_weights_loaded")
        s_wo = sem("out_weights_loaded")
        s_x = [sem(f"x_loaded{b}") for b in range(B)]
        s_gu = sem("gate_up_loaded")
        s_sc = sem("ffn_scales_loaded")
        s_dq = sem("down_q_loaded")
        s_id = sem("identity_ready")
        s_fill = sem("stack_rows_filled")
        s_zero = sem("v_zeroed")
        s_const = sem("constants_set")
        s_proj = sem("projection_full")
        s_projr = sem("projection_read")
        s_vt = sem("v_transposed")
        s_vc = sem("v_placed")
        s_split = sem("qk_residual_ready")
        s_parts = sem("qk_parts_ready")
        s_stk = [sem(f"k_and_q_block0_stacked{b}") for b in range(B)]
        s_stp = sem("rest_stacked0")
        s_stq = [sem(f"q_block1_stacked{b}") for b in range(B)]
        s_rf = sem("ring_full")
        s_rr = {"dve": sem("ring_read_by_dve"), "act": sem("ring_read_by_act")}
        s_mxc = sem("maxima_combined")
        s_msp = sem("maxima_split")
        s_mrow = sem("max_parts_ready")
        s_mld = [sem(f"max_rows_in_stack{g}") for g in range(NG)]
        s_scf = sem("scores_full")
        s_exp = sem("exp_done")
        s_av = sem("av_step_done")
        s_ave = sem("av_evacuated")
        s_rec = sem("denominators_inverted")
        s_bn = sem("ln_stats_of_tile")
        s_st = sem("ln_mean_variance_ready")
        s_ve = sem("ln_variance_plus_eps")
        s_rstd = sem("ln_inverse_ready")
        s_x1 = sem("x1_ready")
        s_hi = sem("x1t_high_ready")
        s_lo = sem("x1t_low_ready")
        s_guf = sem("gate_up_full")
        s_a0 = sem("even_group_scaled")
        s_gud = sem("odd_group_added")
        s_gsum = sem("gate_summed")
        s_usum = sem("up_summed")
        s_silu = sem("silu_done")
        s_mul = sem("inner_ready")
        s_mh = sem("inner_high_ready")
        s_ml = sem("inner_low_ready")
        s_df = sem("down_full")
        s_dr = {"dve": sem("down_read_by_dve"), "act": sem("down_read_by_act")}
        s_ya = sem("down_added_by_pool")
        s_tf = sem("results_turned")
        s_tr = sem("results_added")
        s_res = sem("result_ready")
        s_out = sem("output_stored")

        block = ctx.enter_context(nc.Block())

        def ring_at(n):
            first = [("first", AHEAD + 4 * n + j, 0) for j in range(4) if AHEAD + 4 * n + j < FIRST]
            other = []
            f, r = divmod(n + 3, KT)
            if r == 0 and f < NB * NG:
                other.append(("M", f, 0))
            f, r = divmod(n - 9, KT)
            if r == 0 and 0 <= f:
                other.append(("avT", f, 0))
            u, r = divmod(n - STEPS, STEPS)
            if 0 <= u < NB - 1:
                if r == 2:
                    other.append(("attT", u, 0))
                if r in WO_AT:
                    other.append(("wo", u, WO_AT.index(r)))
                if r in X1T_AT:
                    other.append(("x1T", u, X1T_AT.index(r)))
            return first[0:2] + other + first[2:4]

        WO_AT, X1T_AT = (4, 6, 7, 8), (12, 13, 14, 15)
        before = [("first", n, 0) for n in range(AHEAD)]
        before.insert(FG + 5, ("M", 0, 0))

        tail = [("avT", NB * NG - 1, 0), ("attT", NB - 1, 0)] + [("wo", NB - 1, k) for k in range(BT)] \
            + [None, None] + [use for c in range(C) for use in (("x1T", NB - 1, c), None)]

        def tail_at(t):
            return [tail[t]] if 0 <= t < len(tail) and tail[t] else []

        ring_order = before + [use for n in range(ALL) for use in ring_at(n)]
        BEFORE_TAIL = len(ring_order)
        ring_order = ring_order + [use for use in tail if use]
        ring_index = {use: i for i, use in enumerate(ring_order)}

        def ring_bank(*use):
            i = ring_index[use]
            return bank[RING[i % 3] if i < BEFORE_TAIL else 0]

        def ring_count(*use):
            return ring_index[use] + 1

        def reader(use):
            return "act" if use[0] in ("attT", "x1T") else "dve"

        read_counts = []
        for i, use in enumerate(ring_order):
            read_counts.append(1 + sum(reader(other) == reader(use) for other in ring_order[:i]))

        def wait_read(engine, *use):
            engine.wait_ge(s_rr[reader(use)], read_counts[ring_index[use]])

        def wait_ring_read(engine, end):
            for name in ("dve", "act"):
                engine.wait_ge(s_rr[name], sum(reader(use) == name for use in ring_order[:end]))

        def k_slot(engine, b, i, j, done):
            r = (3 * i + j) * E
            engine.dma_start(ks[b][r:r + E, :, :], part[j][HD:2 * HD, :]).then_inc(done, 16)

        def q_slot(engine, b, i, j, block, done):
            r = (3 * i + j) * E
            engine.dma_start(qs[b][r:r + E, block, :, :], part[i][0:HD, block * TB:(block + 1) * TB])\
                  .then_inc(done, 16)

        def down_reader(t, c):
            return "act" if c == 3 or (c == 2 and t % G < 4) or (c == 1 and t % G == 0) else "dve"

        downs = [(t, c) for t in range(TILES) for c in range(C)]
        down_counts, counted = {}, {"dve": 0, "act": 0, "pool": 0}
        for t, c in downs:
            counted[down_reader(t, c)] += 1
            down_counts[t, c] = counted[down_reader(t, c)]
            if down_reader(t, c) == "act" and t % G:
                counted["pool"] += 1
                down_counts[t, c, "pool"] = counted["pool"]

        def wait_down_read(engine, t, c):
            engine.wait_ge(s_dr[down_reader(t, c)], down_counts[t, c])

        def wait_down_added(engine, t, c):
            if (t, c, "pool") in down_counts:
                engine.wait_ge(s_ya, down_counts[t, c, "pool"])
            else:
                wait_down_read(engine, t, c)

        def turn_at(t):
            blk, i = divmod(t, G)
            return (blk - 1, i - LAG) if 1 <= blk < NB and LAG <= i < LAG + BT else None

        @block.sync
        def _(sp):
            def load_xt(b):
                for k in range(2):
                    if b == 0 and k == 0:
                        sp.dma_start(wqk_s[:], wqkT).then_inc(s_wqk, 16)
                    for c in range(C):
                        q0 = (2 * b + k) * TB
                        sp.dma_start(xt[k][:, c, :], xT[c, :, q0:q0 + TB]).then_inc(s_xt[k][c], 16)
                    if b == 0 and k == 0:
                        sp.dma_start(bqk_s[:], bqk).then_inc(s_bqk, 16)

            load_xt(0)
            sp.dma_start(wv_s[:], wvT).then_inc(s_wv, 16)
            sp.dma_start(bv_s[:], bv).then_inc(s_wv, 16)
            sp.wait_ge(s_fill, 2)
            for i in range(3):
                sp.wait_ge(s_parts, i + 1)
                for j in range(2):
                    q_slot(sp, 0, i, j, 0, s_stk[0])
            for j in range(3):
                sp.wait_ge(s_parts, 3 + j + 1)
                for i in range(2):
                    k_slot(sp, 0, i, j, s_stk[0])
            sp.wait_ge(s_proj, 3)
            load_xt(1)
            for i in range(3):
                for j in range(3):
                    q_slot(sp, 0, i, j, 1, s_stq[0])
            sp.dma_start(wo_s[:], woT).then_inc(s_wo, 16)

            def max_rows(f):
                u, g = divmod(f, NG)
                sp.wait_ge(s_mrow, f + 1)
                sp.wait_ge(s_rf, ring_count("first", (f + 1) * FG - 1, 0))
                b, k = divmod(u, N // TB)
                for i in range(3):
                    dst = qs[b][MROW + i:MROW + i + 1, k, g * HG:(g + 1) * HG, :]
                    sp.dma_start(dst, mp[:, f % 2, i, :]).then_inc(s_mld[g], 16)

            max_rows(0)
            sp.dma_start(gs_s[:], gs).then_inc(s_sc, 16)
            sp.dma_start(us_s[:], us).then_inc(s_sc, 16)
            sp.dma_start(ds_s[:], ds).then_inc(s_sc, 16)
            max_rows(1)
            sp.dma_start(x1[:, 0:8, :], x[0:8].rearrange("t p n -> p t n")).then_inc(s_x[0], 16)
            max_rows(2)
            max_rows(3)
            sp.wait_ge(s_stk[1], 16 * 18)
            sp.wait_ge(s_stq[1], 16 * 9)
            sp.wait_ge(s_vt, B)
            sp.dma_start(x1[:, 8:16, :], x[8:16].rearrange("t p n -> p t n")).then_inc(s_x[1], 16)
            for f in range(4, NB * NG):
                max_rows(f)
            for blk in range(NB - 1):
                sp.wait_ge(s_res, BT * (blk + 1))
                sp.dma_start(out[blk * BT:(blk + 1) * BT].rearrange("t p n -> p t n"),
                             x1[:, blk * BT:(blk + 1) * BT, :]).then_inc(s_out, 16)
            for t in range(T // P - BT, T // P):
                sp.wait_ge(s_res, t + 1)
                sp.dma_start(out[t], x1[:, t, :]).then_inc(s_out, 16)
            sp.wait_ge(s_out, 16 * (NB - 1 + BT))

        @block.gpsimd
        def _(pool):
            nc.gpsimd.memset(ident[:], 0.0).then_inc(s_id, 1)
            pool.wait_ge(s_id, 1)
            nc.gpsimd.affine_select(out=ident[:], in_=ident[:], compare_op=ALU.not_equal, fill=1.0, base=0,
                                    pattern=[[-1, P]], channel_multiplier=1).then_inc(s_id, 1)
            pool.wait_ge(s_id, 2)
            def fill(b):
                for k, value in enumerate((MINUS_ONES, 0.0)):
                    if 2 * b + k:
                        pool.wait_ge(s_fill, 2 * b + k)
                    nc.gpsimd.memset(stack[b][64:96, k, :].bitcast(F32), value).then_inc(s_fill, 1)

            fill(0)

            def inverse(n, tiles=slice(0, BT)):
                pool.wait_ge(s_st, n + 1)
                nc.gpsimd.tensor_scalar(veps[:, tiles], mv[:, tiles, 1], EPS, None, ALU.add).then_inc(s_ve, 1)
                pool.wait_ge(s_ve, n + 1)
                nc.gpsimd.tensor_tensor(rstd[:, tiles], veps[:, tiles], mhalf[:, tiles], ALU.pow).then_inc(s_rstd, 1)

            pool.wait_ge(s_fill, 2)
            for i in range(3):
                pool.wait_ge(s_parts, i + 1)
                q_slot(pool, 0, i, 2, 0, s_stp)
            for j in range(3):
                pool.wait_ge(s_parts, 3 + j + 1)
                k_slot(pool, 0, 2, j, s_stp)
            pool.wait_ge(s_stk[0], 16 * 12)
            pool.wait_ge(s_stp, 16 * 6)
            for c in range(C):
                pool.dma_start(wg[:, c, :], gq[c]).then_inc(s_gu, 16)
                pool.dma_start(wu[:, c, :], uq[c]).then_inc(s_gu, 16)
            fill(1)

            pool.wait_ge(s_fill, 4)
            pool.wait_ge(s_projr, 5)
            pool.wait_ge(s_stq[0], 16 * 9)
            nc.gpsimd.tensor_copy(part[0], qkf).then_inc(s_parts, 1)
            pool.wait_ge(s_parts, 7)
            nc.gpsimd.tensor_tensor(res1, qkf, part[0], ALU.subtract).then_inc(s_split, 1)
            pool.wait_ge(s_split, 3)
            nc.gpsimd.tensor_copy(part[1], res1).then_inc(s_parts, 1)
            pool.wait_ge(s_parts, 8)
            nc.gpsimd.tensor_tensor(part[2], res1, part[1], ALU.subtract).then_inc(s_parts, 1)
            pool.wait_ge(s_parts, 9)
            for i in range(3):
                for j in range(3):
                    k_slot(pool, 1, i, j, s_stk[1])
                    q_slot(pool, 1, i, j, 0, s_stk[1])
            for i in range(3):
                for j in range(3):
                    q_slot(pool, 1, i, j, 1, s_stq[1])

            def x1_low(u, c):
                pool.wait_ge(s_hi, u * C + c + 1)
                wait_read(pool, "x1T", u, c)
                nc.gpsimd.tensor_tensor(x1t[u][:, 1, c, :], x32[:, c, :], x1t[u][:, 0, c, :], ALU.subtract)\
                  .then_inc(s_lo, 1)

            for u in range(NB - 1):
                inverse(u)
                for c in range(C):
                    x1_low(u, c)
                if u == 0:
                    pool.wait_ge(s_scf, 2 * ALL // B)
                    for g in range(0, G, G // 2):
                        pool.dma_start(wd[:, g:g + G // 2, :], dq[g:g + G // 2].rearrange("g p n -> p g n"))\
                            .then_inc(s_dq, 16)

            def inner_low(t):
                pool.wait_ge(s_mh, t + 1)
                if t:
                    pool.wait_ge(s_ml, t)
                if t >= NM:
                    pool.wait_ge(s_df, C * (t - NM + 1))
                nc.gpsimd.tensor_tensor(mparts[:, 1, t % NM, :], sg[t % 2], mparts[:, 0, t % NM, :],
                                        ALU.subtract).then_inc(s_ml, 1)

            def sums(t):
                for acc, half, summed, done in ((ag, bg, s_gsum, 3), (au, bu, s_usum, 4)):
                    pool.wait_ge(s_gud, 4 * t + done)
                    nc.gpsimd.tensor_tensor(acc[t % 2], acc[t % 2], half[t % 2], ALU.add).then_inc(summed, 1)

            def add_down(t):
                for c in range(C):
                    if (t, c, "pool") in down_counts:
                        wait_down_read(pool, t, c)
                        wait_down_added(pool, t - 1, c)
                        y = yacc[:, (t // G) % 2, c, :]
                        nc.gpsimd.tensor_tensor(y, yscaled[:, down_counts[t, c, "pool"] % 2, :], y, ALU.add)\
                            .then_inc(s_ya, 1)

            for t in range(TILES + LAG + 1):
                blk, i = divmod(t, G)
                if t == 7:
                    inverse(NB - 1)
                if t > LAG:
                    add_down(t - LAG - 1)
                if 1 <= t <= TILES:
                    inner_low(t - 1)
                if t < TILES:
                    sums(t)
                for use in tail_at(t - 1):
                    if use[0] == "x1T":
                        x1_low(*use[1:])
                if 1 <= blk < NB and i == G - 1:
                    inverse(NB + blk - 1)
            for k in range(BT):
                inverse(2 * NB - 1 + k, slice(k, k + 1))

        @block.scalar
        def _(act):
            def project(b):
                for k in range(2):
                    act.wait_ge(s_proj, 3 * b + k + 1)
                    if b and k == 0:
                        act.wait_ge(s_parts, 6)
                    nc.scalar.activation(qkf[:, k * TB:(k + 1) * TB], bank[k], ACT.Identity, bias=bqk_s[:])\
                      .then_inc(s_projr, 1)
                act.wait_ge(s_proj, 3 * b + 3)
                if b:
                    act.wait_ge(s_vt, b)
                else:
                    act.wait_ge(s_wv, 32)
                nc.scalar.activation(vtmp, bank[2], ACT.Identity, bias=bv_s[:]).then_inc(s_projr, 1)

            def exps(n):
                for pair in range(2):
                    pi = 2 * n + pair
                    act.wait_ge(s_scf, pi + 1)
                    if n >= 2:
                        act.wait_ge(s_av, n - 1)
                    nc.scalar.activation(pbuf[:, pi % 4, :].rearrange("p (a n) -> p a n", a=2),
                                         ps[:, 2 * (pi % 2):2 * (pi % 2) + 2, :], ACT.Exp).then_inc(s_exp, 1)

            def av_out(f):
                act.wait_ge(s_av, (f + 1) * KT)
                if f >= 2:
                    act.wait_ge(s_rf, ring_count("avT", f - 2, 0))
                nc.scalar.activation(avt[:, f % 2, :], bank[AVB], ACT.Copy).then_inc(s_ave, 1)

            def x1_high(u, c):
                act.wait_ge(s_rf, ring_count("x1T", u, c))
                if u == 2:
                    act.wait_ge(s_av, 2 * STEPS)
                nc.scalar.activation(x1t[u][:, 0, c, :], ring_bank("x1T", u, c), ACT.Copy).then_inc(s_hi, 1)
                if u:
                    act.wait_ge(s_lo, C * (u - 1) + c + 1)
                nc.scalar.activation(x32[:, c, :], ring_bank("x1T", u, c), ACT.Copy).then_inc(s_rr["act"], 1)

            def att_out(u):
                act.wait_ge(s_rf, ring_count("attT", u, 0))
                nc.scalar.activation(attT[:], ring_bank("attT", u, 0)[0:KR, :], ACT.Copy).then_inc(s_rr["act"], 1)

            def ring_use(kind, u, k):
                if kind == "x1T":
                    x1_high(u, k)
                if kind == "attT":
                    att_out(u)

            act.wait_ge(s_const, 1)
            nc.scalar.activation(warm[:], mhalf[:, 0:1], ACT.Identity)
            act.wait_ge(s_bqk, 16)
            project(0)
            project(1)
            for n in range(ALL):
                exps(n)
                if n and n % KT == 0:
                    av_out(n // KT - 1)
                for use in ring_at(n):
                    ring_use(*use)
            av_out(NB * NG - 1)

            def silu(t):
                act.wait_ge(s_gsum, t + 1)
                if t >= 2:
                    act.wait_ge(s_ml, t - 1)
                nc.scalar.activation(sg[t % 2], ag[t % 2], ACT.Silu).then_inc(s_silu, 1)

            def inner_high(t):
                act.wait_ge(s_mul, t + 1)
                if t >= NM:
                    act.wait_ge(s_df, C * (t - NM + 1))
                nc.scalar.activation(mparts[:, 0, t % NM, :], sg[t % 2], ACT.Copy).then_inc(s_mh, 1)

            def down_out(t):
                blk, i = divmod(t, G)
                for c in range(C):
                    if down_reader(t, c) != "act":
                        continue
                    act.wait_ge(s_df, C * t + c + 1)
                    if i == 0:
                        dst = yacc[:, blk % 2, c, :]
                        if blk >= 2:
                            act.wait_ge(s_tf, BT * (blk - 1))
                    else:
                        n = down_counts[t, c, "pool"]
                        dst = yscaled[:, n % 2, :]
                        if n > 2:
                            act.wait_ge(s_ya, n - 2)
                    nc.scalar.activation(dst, bank[c], ACT.Copy, scale=ds_s[:, c, i:i + 1]).then_inc(s_dr["act"], 1)

            act.wait_ge(s_sc, 48)
            act.wait_ge(s_av, ALL)

            def scale_group(t, c):
                i = t % G
                for n, (dst, scl) in enumerate((((ag, bg)[c // 2], gs_s), ((au, bu)[c // 2], us_s))):
                    act.wait_ge(s_guf, 8 * t + 2 * c + n + 1)
                    if t >= 2:
                        act.wait_ge(((s_silu, s_mul), (s_gsum, s_usum))[c // 2][n], t - 1)
                    nc.scalar.activation(dst[t % 2], bank[GUB + n], ACT.Copy, scale=scl[:, i, c:c + 1])\
                      .then_inc(s_a0, 1)

            for t in range(TILES + LAG):
                if t < TILES:
                    scale_group(t, 0)
                for use in tail_at(t - 1):
                    ring_use(*use)
                if 1 <= t <= TILES:
                    silu(t - 1)
                if t < TILES:
                    scale_group(t, 2)
                if 1 <= t <= TILES:
                    inner_high(t - 1)
                if t >= LAG:
                    down_out(t - LAG)

        @block.tensor
        def _(pe):
            def projections(b):
                def qk(k, c):
                    pe.wait_ge(s_xt[k][c], 16 * (b + 1))
                    if b and c == 0:
                        pe.wait_ge(s_projr, 3 * b)
                    mm = nc.tensor.matmul(bank[k], wqk_s[:, c, :], xt[k][:, c, :], start=(c == 0), stop=(c == C - 1))
                    if c == C - 1:
                        mm.then_inc(s_proj, 1)

                def v(c):
                    for k in range(2):
                        mm = nc.tensor.matmul(bank[2][k * HD:(k + 1) * HD, :], wv_s[:, c, :], xt[k][:, c, :],
                                              start=(c == 0), stop=(c == C - 1))
                    if c == C - 1:
                        mm.then_inc(s_proj, 1)

                def vt():
                    pe.wait_ge(s_projr, 3 * (b + 1))
                    if b:
                        pe.wait_ge(s_vc, 2 * b)
                    else:
                        pe.wait_ge(s_id, 2)
                    for t in range(BT):
                        mm = nc.tensor.transpose(bank[3][:, t * P:(t + 1) * P], vtmp[:, t * P:(t + 1) * P], ident[:])
                    mm.then_inc(s_vt, 1)

                return [(qk, k, c) for k in range(2) for c in range(C)] + [(v, c) for c in range(C)] + [(vt,)]

            def first_pass(n):
                u, r = divmod(n, H * BT * 2)
                h, r = divmod(r, BT * 2)
                qt, half = divmod(r, 2)
                b, k = divmod(u, N // TB)
                if n == 0:
                    pe.wait_ge(s_stk[0], 16 * 12)
                    pe.wait_ge(s_stp, 16 * 6)
                elif n % (4 * FG) == 0:
                    pe.wait_ge(s_stk[b], 16 * 18)
                elif n % (2 * FG) == 0:
                    pe.wait_ge(s_stq[b], 16 * 9)
                nc.tensor.matmul(ring_bank("first", n, 0), qs[b][:, k, h, qt * P:(qt + 1) * P],
                                 ks[b][:, h, half * TB:(half + 1) * TB], start=True, stop=True).then_inc(s_rf, 1)

            def ring_use(kind, u, k):
                i = ring_index[kind, u, k]
                if i >= 3:
                    wait_read(pe, *ring_order[i - (3 if i < BEFORE_TAIL else 1)])
                if (kind, u, k) == tail[0]:
                    pe.wait_ge(s_exp, 2 * ALL)
                dst = ring_bank(kind, u, k)
                if kind == "first":
                    first_pass(u)
                    return
                if kind == "M":
                    pe.wait_ge(s_mxc, u + 1)
                    mm = nc.tensor.transpose(dst[0:HG * BT, 0:P], mx[:, u % 2, :], ident[:])
                elif kind == "avT":
                    pe.wait_ge(s_ave, u + 1)
                    for t in range(BT):
                        mm = nc.tensor.transpose(dst[:, t * P:(t + 1) * P], avt[:, u % 2, t * P:(t + 1) * P], ident[:])
                elif kind == "attT":
                    wait_read(pe, "avT", NG * u + 1, 0)
                    for t in range(BT):
                        mm = nc.tensor.transpose(dst[0:KR, t * P:(t + 1) * P], att[:, t, :], ident[:])
                elif kind == "wo":
                    if k == 0:
                        pe.wait_ge(s_wo, 16)
                        wait_read(pe, "attT", u, 0)
                    mm = nc.tensor.matmul(dst, attT[:, k * P:(k + 1) * P], wo_s[:], start=True, stop=True)
                else:
                    pe.wait_ge(s_x1, u + 1)
                    for t in range(BT):
                        mm = nc.tensor.transpose(dst[:, t * P:(t + 1) * P], x1[:, u * BT + t, k * P:(k + 1) * P],
                                                 ident[:])
                mm.then_inc(s_rf, 1)

            def scores(n, pair):
                u, s = divmod(n, STEPS)
                g, kt = divmod(s, KT)
                b, k = divmod(u, N // TB)
                pi = 2 * n + pair
                if kt == 0 and pair == 0:
                    pe.wait_ge(s_mld[g], 16 * 3 * (u + 1))
                if pi >= 2:
                    pe.wait_ge(s_exp, pi - 1)
                elif pi == 0:
                    pe.wait_ge(s_vc, 2 * B)
                for j in range(2):
                    h = g * HG + 2 * pair + j
                    mm = nc.tensor.matmul(bank[2 * (pi % 2) + j], ks[b][:, h, kt * P:(kt + 1) * P],
                                          qs[b][:, k, h, :], start=True, stop=True)
                mm.then_inc(s_scf, 1)

            def av(n):
                u, s = divmod(n, STEPS)
                g, kt = divmod(s, KT)
                b = u * TB // N
                pe.wait_ge(s_exp, 2 * n + 2)
                if n == 0:
                    pe.wait_ge(s_vc, 2 * B)
                if kt == 0 and n:
                    pe.wait_ge(s_ave, n // KT)
                for j in range(HG):
                    mm = nc.tensor.matmul(bank[AVB][j * VC:(j + 1) * VC, :], vst[b][:, kt, g * HG + j, :],
                                          pbuf[:, (2 * n + j // 2) % 4, (j % 2) * TB:(j % 2 + 1) * TB],
                                          start=(kt == 0), stop=(kt == KT - 1))
                mm.then_inc(s_av, 1)

            def piece(p):
                p[0](*p[1:])

            pe.wait_ge(s_wqk, 16)
            for n, p in enumerate(projections(0)):
                if n == 2 * C:
                    pe.wait_ge(s_wv, 32)
                piece(p)
            later = projections(1)
            for n, use in enumerate(before):
                ring_use(*use)
                if n >= 8 and n % 2 and later:
                    piece(later.pop(0))
            for n in range(ALL):
                uses = ring_at(n)
                late = max(1, len(uses) - (2 if len(uses) >= 4 else 0))
                scores(n, 0)
                for use in uses[0:1]:
                    ring_use(*use)
                scores(n, 1)
                for use in uses[1:late + 1]:
                    ring_use(*use)
                if n:
                    av(n - 1)
                for use in uses[late + 1:]:
                    ring_use(*use)
            av(ALL - 1)

            def down(t, c):
                i = t % G
                if c == 0:
                    pe.wait_ge(s_ml, t + 1)
                if t == 0 and c == 0:
                    pe.wait_ge(s_dq, 32)
                if t:
                    wait_down_read(pe, t - 1, c)
                if c == 0:
                    for use in tail_at(t + LAG - 1):
                        wait_read(pe, *use)
                    if turn_at(t + LAG - 1):
                        blk, k = turn_at(t + LAG - 1)
                        pe.wait_ge(s_tr, BT * blk + k + 1)
                for a in range(2):
                    mm = nc.tensor.matmul(bank[c], wd[:, i, c * P:(c + 1) * P], mparts[:, a, t % NM, :],
                                          start=(a == 0), stop=(a == 1))
                mm.then_inc(s_df, 1)

            def turn(blk, k, dst):
                for c in range(C):
                    wait_down_added(pe, blk * G + G - 1, c)
                    y = yacc[:, blk % 2, c, k * P:(k + 1) * P]
                    mm = nc.tensor.transpose(dst[:, c * P:(c + 1) * P], y, ident[:])
                mm.then_inc(s_tf, 1)

            pe.wait_ge(s_gu, 16 * 2 * C)
            wait_ring_read(pe, BEFORE_TAIL)
            for t in range(TILES + LAG):
                blk, i = divmod(t, G)
                if t < TILES and i == 0:
                    pe.wait_ge(s_hi, C * (blk + 1))
                    pe.wait_ge(s_lo, C * (blk + 1))
                for j in range(8):
                    if t < TILES:
                        c, n = divmod(j, 2)
                        w = (wg, wu)[n]
                        if j >= 4 or t:
                            pe.wait_ge((s_a0, s_gud)[c % 2], 4 * t + 2 * (c // 2) + n - 1)
                        elif j == AVB - GUB:
                            pe.wait_ge(s_ave, NB * NG)
                        for a in range(2):
                            mm = nc.tensor.matmul(bank[GUB + j % 4], w[:, c, i * P:(i + 1) * P], x1t[blk][:, a, c, :],
                                                  start=(a == 0), stop=(a == 1))
                        mm.then_inc(s_guf, 1)
                    if t >= LAG and j in (3, 7):
                        down(t - LAG, j // 2 - 1)
                        down(t - LAG, j // 2)
                if t >= LAG and (tail_at(t) or turn_at(t)):
                    wait_down_read(pe, t - LAG, 0)
                for use in tail_at(t):
                    ring_use(*use)
                if turn_at(t):
                    turn(*turn_at(t), bank[0])
            for k in range(BT):
                wait_down_read(pe, TILES - 1, k)
                turn(NB - 1, k, bank[k])

        @block.vector
        def _(dve):
            nc.vector.memset(mhalf[:], -0.5).then_inc(s_const, 1)
            nc.vector.memset(att[:], 0.0).then_inc(s_zero, 1)
            nc.vector.memset(arena[:, 2:4, :], 0.0).then_inc(s_zero, 1)
            dve.wait_ge(s_zero, 2)
            nc.vector.memset(att[:, :, HD:HD + 1], 1.0)
            for b in range(B):
                nc.vector.memset(vst[b][:, :, :, E:E + 1], float(HD) ** 0.5)

            def split(k):
                cols = slice(k * TB, (k + 1) * TB)
                dve.wait_ge(s_projr, k + 1)
                nc.vector.tensor_copy(part[0][:, cols], qkf[:, cols]).then_inc(s_parts, 1)
                dve.wait_ge(s_parts, 3 * k + 1)
                nc.vector.tensor_tensor(res1[:, cols], qkf[:, cols], part[0][:, cols], ALU.subtract)\
                  .then_inc(s_split, 1)
                dve.wait_ge(s_split, k + 1)
                nc.vector.tensor_copy(part[1][:, cols], res1[:, cols]).then_inc(s_parts, 1)
                dve.wait_ge(s_parts, 3 * k + 2)
                nc.vector.tensor_tensor(part[2][:, cols], res1[:, cols], part[1][:, cols], ALU.subtract)\
                  .then_inc(s_parts, 1)

            def place_v(b):
                dve.wait_ge(s_vt, b + 1)
                for k in range(2):
                    src = bank[3].rearrange("p (t k h e) -> p t k h e", t=BT, k=2, h=H)[:, :, k, :, :]
                    nc.vector.tensor_copy(vst[b][:, k * BT:(k + 1) * BT, :, 0:E], src).then_inc(s_vc, 1)

            def reduce(n):
                f, r = divmod(n, HG * BT * 2)
                qh, half = divmod(r, 2)
                dve.wait_ge(s_rf, ring_count("first", n, 0))
                nc.vector.tensor_reduce(mxh[:, f % 2, qh, half:half + 1], ring_bank("first", n, 0), AX.X, ALU.max)\
                  .then_inc(s_rr["dve"], 1)

            def combine(f):
                wait_read(dve, "first", (f + 1) * FG - 1, 0)
                if f >= 2:
                    dve.wait_ge(s_rf, ring_count("M", f - 2, 0))
                nc.vector.tensor_tensor(mx[:, f % 2, :], mxh[:, f % 2, :, 0], mxh[:, f % 2, :, 1], ALU.max)\
                  .then_inc(s_mxc, 1)

            def split_max(f):
                dve.wait_ge(s_rf, ring_count("M", f, 0))
                if f >= 2:
                    dve.wait_ge(s_mld[f % NG], 16 * 3 * (f // NG))
                rows = ring_bank("M", f, 0)[0:HG * BT, 0:P]
                nc.vector.tensor_copy(mp[:, f % 2, 0, :], rows).then_inc(s_msp, 1)
                dve.wait_ge(s_msp, 3 * f + 1)
                nc.vector.tensor_tensor(mres[:, 0, :], rows, mp[:, f % 2, 0, :], ALU.subtract).then_inc(s_rr["dve"], 1)
                wait_read(dve, "M", f, 0)
                nc.vector.tensor_copy(mp[:, f % 2, 1, :], mres[:, 0, :]).then_inc(s_msp, 1)
                dve.wait_ge(s_msp, 3 * f + 2)
                nc.vector.tensor_tensor(mres[:, 1, :], mres[:, 0, :], mp[:, f % 2, 1, :], ALU.subtract)\
                  .then_inc(s_msp, 1)
                dve.wait_ge(s_msp, 3 * f + 3)
                nc.vector.tensor_copy(mp[:, f % 2, 2, :], mres[:, 1, :]).then_inc(s_mrow, 1)

            def normalise(f):
                dve.wait_ge(s_rf, ring_count("avT", f, 0))
                g = f % NG
                src = ring_bank("avT", f, 0).rearrange("p (t h v) -> p t h v", t=BT, h=HG)
                nc.vector.reciprocal(rec[:], src[:, :, :, E]).then_inc(s_rec, 1)
                dve.wait_ge(s_rec, f + 1)
                dst = att[:, :, g * HG * E:(g + 1) * HG * E].rearrange("p t (h e) -> p t h e", h=HG)
                nc.vector.tensor_tensor(dst, src[:, :, :, 0:E], rec[:].unsqueeze(3).to_broadcast([P, BT, HG, E]),
                                        ALU.mult).then_inc(s_rr["dve"], 1)

            def add_attention(u, t):
                dve.wait_ge(s_rf, ring_count("wo", u, t))
                if t == 0:
                    dve.wait_ge(s_x[u * TB // N], 16)
                x1_t = x1[:, u * BT + t, :]
                nc.vector.tensor_tensor(x1_t, ring_bank("wo", u, t), x1_t, ALU.add).then_inc(s_rr["dve"], 1)
                wait_read(dve, "wo", u, t)
                nc.vector.bn_stats(st[:, t, :], x1_t).then_inc(s_bn, 1)

            def mean_variance(n):
                dve.wait_ge(s_bn, BT * (n + 1))
                for t in range(BT):
                    op = nc.vector.bn_aggr(mv[:, t, :], st[:, t, :])
                op.then_inc(s_st, 1)

            def apply(n, done, tiles=range(BT)):
                blk = n % NB
                dve.wait_ge(s_rstd, n + 1)
                for t in tiles:
                    x1_t = x1[:, blk * BT + t, :]
                    op = nc.vector.tensor_scalar(x1_t, x1_t, mv[:, t, 0:1], rstd[:, t:t + 1], ALU.subtract, ALU.mult)
                    if done is s_res:
                        op.then_inc(s_res, 1)
                if done is not s_res and t == BT - 1:
                    op.then_inc(done, 1)

            split(0)
            split(1)
            place_v(0)
            def ring_use(kind, u, k):
                if kind == "first":
                    reduce(u)
                    if (u + 1) % FG == 0:
                        combine(u // FG)
                elif kind == "M":
                    split_max(u)
                elif kind == "avT":
                    normalise(u)
                elif kind == "wo":
                    add_attention(u, k)

            for n, use in enumerate(before):
                ring_use(*use)
                if n == AHEAD - 2:
                    place_v(1)
            for n in range(ALL):
                for use in ring_at(n):
                    ring_use(*use)
                if n > STEPS and n % STEPS == 8:
                    mean_variance(n // STEPS - 1)
                if n > STEPS and n % STEPS in (9, 10, 11):
                    apply(n // STEPS - 1, s_x1, ([0], [1], [2, 3])[n % STEPS - 9])

            def product(t):
                dve.wait_ge(s_silu, t + 1)
                dve.wait_ge(s_usum, t + 1)
                nc.vector.tensor_tensor(sg[t % 2], sg[t % 2], au[t % 2], ALU.mult).then_inc(s_mul, 1)

            def down_out(t, c):
                if down_reader(t, c) != "dve":
                    return
                blk, i = divmod(t, G)
                dve.wait_ge(s_df, C * t + c + 1)
                y, scl = yacc[:, blk % 2, c, :], ds_s[:, c, i:i + 1]
                if t == 0:
                    dve.wait_ge(s_sc, 48)
                if i == 0:
                    if blk >= 2:
                        dve.wait_ge(s_tf, BT * (blk - 1))
                    op = nc.vector.tensor_scalar(y, bank[c], scl, None, ALU.mult)
                else:
                    wait_down_added(dve, t - 1, c)
                    op = nc.vector.scalar_tensor_tensor(out=y, in0=bank[c], scalar=scl, in1=y,
                                                        op0=ALU.mult, op1=ALU.add)
                op.then_inc(s_dr["dve"], 1)

            def add_result(blk, k, src):
                n = BT * blk + k
                dve.wait_ge(s_tf, n + 1)
                nc.vector.tensor_tensor(x1[:, n, :], src, x1[:, n, :], ALU.add).then_inc(s_tr, 1)
                dve.wait_ge(s_tr, n + 1)
                nc.vector.bn_stats(st[:, k, :], x1[:, n, :]).then_inc(s_bn, 1)

            for t in range(TILES + LAG):
                blk, i = divmod(t, G)
                for use in tail_at(t - 1):
                    ring_use(*use)
                if t and turn_at(t - 1):
                    add_result(*turn_at(t - 1), bank[0])
                for c in (1, 3):
                    for n, (acc, scl) in enumerate((((ag, bg)[c // 2], gs_s), ((au, bu)[c // 2], us_s))):
                        if t < TILES:
                            dve.wait_ge(s_guf, 8 * t + 2 * c + n + 1)
                            dve.wait_ge(s_a0, 4 * t + c + n)
                            nc.vector.scalar_tensor_tensor(out=acc[t % 2], in0=bank[GUB + 2 + n],
                                                           scalar=scl[:, i, c:c + 1], in1=acc[t % 2],
                                                           op0=ALU.mult, op1=ALU.add).then_inc(s_gud, 1)
                    if t >= LAG:
                        down_out(t - LAG, c - 1)
                        down_out(t - LAG, c)
                    if c == (3 if t == TILES else 1) and 1 <= t <= TILES:
                        product(t - 1)
                if t == 6:
                    mean_variance(NB - 1)
                if t == 7:
                    apply(NB - 1, s_x1)
                if 1 <= blk < NB and i == LAG + BT:
                    mean_variance(NB + blk - 1)
                if blk >= 2 and i < 2:
                    apply(NB + blk - 2, s_res, range(2 * i, 2 * i + 2))
            for k in range(BT):
                add_result(NB - 1, k, bank[k])
                dve.wait_ge(s_bn, BT * (2 * NB - 1) + k + 1)
                nc.vector.bn_aggr(mv[:, k, :], st[:, k, :]).then_inc(s_st, 1)
            for k in range(BT):
                x1_t = x1[:, (NB - 1) * BT + k, :]
                dve.wait_ge(s_rstd, 2 * NB + k)
                nc.vector.tensor_scalar(x1_t, x1_t, mv[:, k, 0:1], rstd[:, k:k + 1], ALU.subtract, ALU.mult)\
                  .then_inc(s_res, 1)


def kernel(L0_attn_x, L0_attn_Wqk_w, L0_attn_Wqk_b, L0_attn_Wv_w, L0_attn_Wv_b, L0_attn_Wo_w, L0_attn_Wo_b,
           L0_ffn_gate_q, L0_ffn_gate_s, L0_ffn_up_q, L0_ffn_up_s, L0_ffn_down_q, L0_ffn_down_s):
    import concourse.bacc as bacc
    from concourse.bass_utils import run_bass_kernel_spmd

    x = np.asarray(L0_attn_x).reshape(T, D)
    wqk, bqk = np.asarray(L0_attn_Wqk_w), np.asarray(L0_attn_Wqk_b)
    wqk = wqk.reshape(H, E, 2, D).transpose(2, 1, 0, 3).reshape(2 * HD, D)
    bqk = bqk.reshape(H, E, 2).transpose(2, 1, 0).reshape(2 * HD, 1)
    bv = np.asarray(L0_attn_Wv_b)
    wo = np.zeros((KR, D), np.float32)
    wo[0:HD] = np.asarray(L0_attn_Wo_w).T
    wo[HD] = np.asarray(L0_attn_Wo_b)
    arrays = {
        "x": x.reshape(T // P, P, D),
        "xT": x.T.reshape(C, P, T),
        "wqkT": wqk.T.reshape(C, P, 2 * HD).transpose(1, 0, 2),
        "bqk": bqk,
        "wvT": np.asarray(L0_attn_Wv_w).T.reshape(C, P, HD).transpose(1, 0, 2),
        "bv": np.concatenate([bv, bv]).reshape(2 * HD, 1),
        "woT": wo,
        "gq": np.asarray(L0_ffn_gate_q).T.reshape(C, P, I),
        "gs": np.asarray(L0_ffn_gate_s).reshape(G, P, C).transpose(1, 0, 2),
        "uq": np.asarray(L0_ffn_up_q).T.reshape(C, P, I),
        "us": np.asarray(L0_ffn_up_s).reshape(G, P, C).transpose(1, 0, 2),
        "dq": np.asarray(L0_ffn_down_q).T.reshape(G, P, D),
        "ds": np.asarray(L0_ffn_down_s).reshape(C, P, G).transpose(1, 0, 2),
    }
    arrays = {name: np.ascontiguousarray(a) for name, a in arrays.items()}
    nc = bacc.Bacc("TRN2", target_bir_lowering=False, num_devices=1)
    args = [nc.dram_tensor(name, a.shape, mybir.dt.from_np(a.dtype), kind="ExternalInput").ap()
            for name, a in arrays.items()]
    out = nc.dram_tensor("out", (T // P, P, D), F32, kind="ExternalOutput").ap()
    build(nc, *args, out)
    r = run_bass_kernel_spmd(nc, [arrays], core_ids=[0])
    return r.results[0]["out"].reshape(B, N, D)
```
